# Optimizing a Trainium2 kernel written in Bass

```python
import numpy as np
import jax
import jax.numpy as jnp

def _softmax(x, axis=-1):
    return jax.nn.softmax(x, axis=axis)

def _gelu(x):
    return jax.nn.gelu(x, approximate=True)

def _silu(x):
    return jax.nn.silu(x)

def _sigmoid(x):
    return jax.nn.sigmoid(x)

def _layernorm(x, axis=-1, eps=1e-05):
    m = jnp.mean(x, axis=axis, keepdims=True)
    v = jnp.var(x, axis=axis, keepdims=True)
    return (x - m) / jnp.sqrt(v + eps)

def _scatter_add(tgt, idx, src, axis=0):
    return tgt.at[idx].add(src)

def _segment_sum(src, seg, n):
    return jax.ops.segment_sum(src, seg, n)
kernel_name = 'mk_adj_resnorm_d1_adj_r2_bd391c'

def setup_inputs(seed: int=0):
    np.random.seed(seed)
    _w = jnp.asarray

    def _rec_inputs():
        import jax
        import jax.numpy as jnp
        _gk = jax.random.key(seed)
        x = -0.0004039 + 1 * jax.random.normal(jax.random.fold_in(_gk, 1), (64, 128, 384), jnp.float32)
        _w = (1.0 + jnp.arange(128, dtype=jnp.float32)) ** (-0.5)
        _w = _w / _w.mean()
        _pij = jnp.clip(0.125 * _w[:, None] * _w[None, :], 0.0, 1.0)
        _a = jax.random.uniform(jax.random.fold_in(_gk, 2), (64, 128, 128)) < _pij
        _af = _a.astype(jnp.float32)
        adj = _af
        return (x, adj)
    x, adj = _rec_inputs()

    def _L0_gnn_setup():
        import jax, jax.numpy as jnp
        import numpy as np
        B, S, H, L = (32, 256, 384, 2)

        def _layer_norm(z, a, b, eps=0.001):
            mu = jnp.mean(z, axis=-1, keepdims=True)
            sigma = jnp.std(z, axis=-1, keepdims=True, ddof=1)
            return (z - mu) / (sigma + eps) * a + b
        key = jax.random.key(seed)
        ks = jax.random.split(key, 6)
        hidden_state = jax.random.normal(ks[0], (B, S, H), dtype=jnp.float32)
        adjacency_matrix = (jax.random.uniform(ks[1], (B, S, S)) < 0.2).astype(jnp.float32)
        W_left = 0.05 * jax.random.normal(ks[2], (L, H, H), dtype=jnp.float32)
        W_right = 0.05 * jax.random.normal(ks[3], (L, H, H), dtype=jnp.float32)
        W_lin = 0.05 * jax.random.normal(ks[4], (L, H, H), dtype=jnp.float32)
        b_lin = jnp.zeros((L, H), dtype=jnp.float32)
        ln_a = jnp.ones((L, H), dtype=jnp.float32)
        ln_b = jnp.zeros((L, H), dtype=jnp.float32)
        return {'hidden_state': hidden_state, 'adjacency_matrix': adjacency_matrix, 'W_left': W_left, 'W_right': W_right, 'W_lin': W_lin, 'b_lin': b_lin, 'ln_a': ln_a, 'ln_b': ln_b}
    _L0_gnn_all = _L0_gnn_setup()
    _L0_gnn_in = {k: v for k, v in _L0_gnn_all.items() if k in ('W_left', 'W_right', 'W_lin', 'b_lin', 'ln_a', 'ln_b')}
    del _L0_gnn_all
    return {'x': x, 'adj': adj, 'L0_gnn_W_left': _L0_gnn_in['W_left'], 'L0_gnn_W_right': _L0_gnn_in['W_right'], 'L0_gnn_W_lin': _L0_gnn_in['W_lin'], 'L0_gnn_b_lin': _L0_gnn_in['b_lin'], 'L0_gnn_ln_a': _L0_gnn_in['ln_a'], 'L0_gnn_ln_b': _L0_gnn_in['ln_b']}

def reference(x, adj, L0_gnn_W_left, L0_gnn_W_right, L0_gnn_W_lin, L0_gnn_b_lin, L0_gnn_ln_a, L0_gnn_ln_b):
    import jax
    import jax.numpy as jnp

    def _L0_gnn_ref(hidden_state, adjacency_matrix, W_left, W_right, W_lin, b_lin, ln_a, ln_b):
        import jax, jax.numpy as jnp
        import numpy as np
        B, S, H, L = (32, 256, 384, 2)

        def _layer_norm(z, a, b, eps=0.001):
            mu = jnp.mean(z, axis=-1, keepdims=True)
            sigma = jnp.std(z, axis=-1, keepdims=True, ddof=1)
            return (z - mu) / (sigma + eps) * a + b
        temper = float(np.sqrt(H))
        adj = adjacency_matrix
        adj_tri = jnp.triu(adj, k=1)
        diag_mask = jnp.triu(adj, k=0) - adj_tri
        h = hidden_state
        for l in range(L):
            m_left = jnp.einsum('bsh,oh->bso', h, W_left[l])
            m_right = jnp.einsum('bsh,oh->bso', h, W_right[l])
            u_left = jnp.einsum('bih,bjh->bij', h, m_left) / temper
            u_right = jnp.einsum('bih,bjh->bij', h, m_right) / temper
            u = u_left * adj_tri + u_left * diag_mask + u_right * jnp.swapaxes(adj_tri, 1, 2)
            delta_exp_u = jnp.exp(u) * adj
            attention = delta_exp_u / (jnp.sum(delta_exp_u, axis=2, keepdims=True) + 1e-10)
            h_lin = jnp.einsum('bsh,oh->bso', h, W_lin[l]) + b_lin[l]
            ctx = jnp.matmul(attention, h_lin)
            h = jax.nn.relu(_layer_norm(ctx, ln_a[l], ln_b[l]))
        return h
    x = _layernorm(x + _L0_gnn_ref(x, adj, L0_gnn_W_left, L0_gnn_W_right, L0_gnn_W_lin, L0_gnn_b_lin, L0_gnn_ln_a, L0_gnn_ln_b), axis=-1)
    return x

_drawn_inputs = setup_inputs


def setup_inputs(seed=0):
    import zlib

    import numpy as np

    out = dict(_drawn_inputs(seed))
    spreads = {'L0_gnn_b_lin': (0.0, 0.1), 'L0_gnn_ln_a': (1.0, 0.2), 'L0_gnn_ln_b': (0.0, 0.1)}
    factors = {}
    for name, (base, spread) in spreads.items():
        noise = np.random.default_rng([zlib.crc32(name.encode()), seed]).standard_normal(out[name].shape)
        drawn = base * np.exp(spread * noise) if base else spread * noise
        out[name] = jnp.asarray(drawn.astype(out[name].dtype))
    for name, factor in factors.items():
        out[name] = (out[name] * factor).astype(out[name].dtype)
    return out
```

```python
from contextlib import ExitStack
from math import sqrt

import concourse.bass as bass
from concourse import mybir

ALU = mybir.AluOpType
ACT = mybir.ActivationFunctionType
F32 = mybir.dt.float32
F32R = mybir.dt.float32r

P = 128


def gnn_resnorm_kernel(nc, x, adj, w_left, w_right, w_lin, b_lin, ln_a, ln_b, out):
    B, S, H = x.shape
    L = w_left.shape[0]
    G = 4
    KC = H // P
    NO = 2 * KC
    PAIRS = B // G // 2
    HV = H + 2
    assert S == P and L == 2 and B % (2 * G) == 0
    SCALE = 1.0 / sqrt(H)
    BESSEL = sqrt(H / (H - 1))

    x_g = x.rearrange("(g q) s h -> g s q h", q=G)
    adj_g = adj.rearrange("(g q) s t -> g s q t", q=G)
    out_g = out.rearrange("(g q) s h -> g s q h", q=G)

    with ExitStack() as ctx:
        def sb(name, shape, dt=F32):
            return ctx.enter_context(nc.sbuf_tensor(name, shape, dt))

        def sem(name):
            return ctx.enter_context(nc.semaphore(name))

        w_hi = [[sb(f"w{d}{l}_hi", [P, KC, H], F32R) for d in "LR"] for l in range(L)]
        w_lo = [[sb(f"w{d}{l}_lo", [P, KC, H], F32R) for d in "LR"] for l in range(L)]
        wlin_hi = [sb(f"wlinT{l}_hi", [P, KC, H], F32R) for l in range(L)]
        wlin_lo = [sb(f"wlinT{l}_lo", [P, KC, H], F32R) for l in range(L)]
        hT_hi = [sb(f"hT_hi{i}", [P, KC, G, P], F32R) for i in range(2)]
        hT_lo = [sb(f"hT_lo{i}", [P, KC, G, P], F32R) for i in range(2)]
        n_hi = sb("n_hi", [P, KC, G, 2, P], F32R)
        n_lo = sb("n_lo", [P, KC, G, 2, P], F32R)
        v_hi = [sb(f"v_hi{i}", [P, G, HV], F32R) for i in range(2)]
        v_lo = [sb(f"v_lo{i}", [P, G, HV], F32R) for i in range(2)]
        e_hi = sb("e_hi", [P, G, P], F32R)
        e_lo = sb("e_lo", [P, G, P], F32R)
        um = sb("um", [P, 2, 2, 2, P])
        ex = sb("ex", [P, 2, 2, P])
        vb = sb("vb", [P, 2, H])
        h_full = sb("h_full", [P, 2, G * P])
        adjT = [sb(f"adjT{s}", [P, G, P]) for s in range(2)]
        mask = [sb(f"mask{s}", [P, G, 2, P]) for s in range(2)]
        adj_in = [sb(f"adj_in{s}", [P, G, P]) for s in range(2)]
        x_in = [sb(f"x_in{s}", [P, G, H]) for s in range(2)]
        x_res = sb("x_res", [P, G, H])
        c_sb = [sb(f"c_sb{i}", [P, G, HV]) for i in range(2)]
        y_out = sb("y_out", [P, G, H])
        b_bc = sb("b_bc", [P, L, H])
        a1_bc = sb("a1_bc", [P, H])
        b1_bc = sb("b1_bc", [P, H])
        a0_col = sb("a0_col", [P, KC])
        b0_col = sb("b0_col", [P, KC])
        ident = sb("ident", [P, P])
        side_of = sb("side_of", [P, 2, P])
        half = sb("half", [P, G])
        mhalf = sb("mhalf", [P, G])
        bn = sb("bn", [P, G, 6])
        mv = sb("mv", [P, G, 2])
        std = sb("std", [P, G])
        den = sb("den", [P, G])
        den2 = sb("den2", [P, G])
        gain = sb("gain", [P, G])
        shift = sb("shift", [P, G])
        fbn = sb("fbn", [P, G, 6])
        fmv = sb("fmv", [P, G, 2])
        fvar = sb("fvar", [P, G])
        rstd = sb("rstd", [P, G])

        def bank(name):
            return ctx.enter_context(nc.psum_tensor(name, [P, 512], F32))

        ps_v = [bank(f"ps_v{i}") for i in range(2)]
        ps_n = [bank(f"ps_n{i}") for i in range(2)]
        ps_u = [bank(f"ps_u{i}") for i in range(2)]
        ps_c = bank("ps_c")
        ps_t = bank("ps_t")

        d_x = [sem(f"d_x{s}") for s in range(2)]
        d_adj = [sem(f"d_adj{s}") for s in range(2)]
        d_xres = sem("d_xres")
        d_out = sem("d_out")
        d_w = [sem(f"d_w{i}") for i in range(3 * L)]
        d_small = sem("d_small")
        ident0 = sem("ident0")
        ident_ready = sem("ident_ready")
        dve_const = sem("dve_const")
        tri_ready = sem("tri_ready")
        pe_w = sem("pe_w")
        act_whi = sem("act_whi")
        dve_wlo = sem("dve_wlo")
        pe_t = sem("pe_t")
        pe_at = sem("pe_at")
        pe_v = sem("pe_v")
        pe_n = sem("pe_n")
        pe_u = sem("pe_u")
        pe_c = sem("pe_c")
        act_h = sem("act_h")
        act_thi = sem("act_thi")
        act_at = sem("act_at")
        act_vhi = sem("act_vhi")
        act_nhi = sem("act_nhi")
        act_exp = sem("act_exp")
        act_ehi = sem("act_ehi")
        act_c = sem("act_c")
        act_norm = sem("act_norm")
        dve_tlo = sem("dve_tlo")
        dve_vb = sem("dve_vb")
        dve_nlo = sem("dve_nlo")
        dve_um = sem("dve_um")
        dve_us = sem("dve_us")
        dve_bn = sem("dve_bn")
        dve_mv = sem("dve_mv")
        dve_den = sem("dve_den")
        dve_den2 = sem("dve_den2")
        dve_gain = sem("dve_gain")
        dve_shift = sem("dve_shift")
        dve_y = sem("dve_y")
        dve_fbn = sem("dve_fbn")
        dve_fmv = sem("dve_fmv")
        dve_fvar = sem("dve_fvar")
        dve_out = sem("dve_out")
        pool_vlo = sem("pool_vlo")
        pool_e = sem("pool_e")
        pool_elo = sem("pool_elo")
        pool_std = sem("pool_std")
        pool_rstd = sem("pool_rstd")
        pool_za = sem("pool_za")
        pool_z = sem("pool_z")
        pool_mask = sem("pool_mask")

        def need(eng, s, n):
            if not isinstance(n, int) or n > 0:
                eng.wait_ge(s, n)

        def run(eng, step):
            step(-1, 3, False, True, False, False)
            for u in range(4):
                step(0, u, True, True, u > 0, False)
            with eng.Fori(1, PAIRS - 1) as pair:
                for u in range(4):
                    step(pair, u, True, True, True, u < 2)
            for u in range(4):
                step(PAIRS - 1, u, True, u < 3, True, u < 2)
            step(PAIRS, 0, False, False, True, True)
            step(PAIRS, 1, False, False, False, True)

        block = ctx.enter_context(nc.Block())

        @block.sync
        def _(sp):
            w_src = [w_lin[0], w_left[0], w_right[0], w_lin[1], w_left[1], w_right[1]]
            stage = [c_sb[0][:, 0:3, 0:H], c_sb[1][:, 0:3, 0:H], y_out[:, 0:3, :], x_res[:, 0:3, :],
                     c_sb[1][:, 0:3, 0:H], y_out[:, 0:3, :]]

            def load_w(i):
                sp.dma_start(stage[i], w_src[i].rearrange("(c p) h -> p c h", p=P)).then_inc(d_w[i], 16)

            sp.dma_start(x_in[0][:, :, :], x_g[0]).then_inc(d_x[0], 16)
            load_w(0)
            load_w(1)
            load_w(2)
            sp.dma_start(adj_in[0][:, :, :], adj_g[0]).then_inc(d_adj[0], 16)
            sp.dma_start(b_bc[:, :, :], b_lin.rearrange("(o l) h -> o l h", o=1).to_broadcast([P, L, H]))\
                .then_inc(d_small, 16)
            with nc.allow_non_contiguous_dma(reason="384 words, once"):
                sp.dma_start(a0_col[:, :], ln_a[0].rearrange("(c p) -> p c", p=P)).then_inc(d_small, 16)
                sp.dma_start(b0_col[:, :], ln_b[0].rearrange("(c p) -> p c", p=P)).then_inc(d_small, 16)
            sp.dma_start(a1_bc[:, :], ln_a[1:2].to_broadcast([P, H])).then_inc(d_small, 16)
            sp.dma_start(b1_bc[:, :], ln_b[1:2].to_broadcast([P, H])).then_inc(d_small, 16)
            sp.dma_start(x_in[1][:, :, :], x_g[1]).then_inc(d_x[1], 16)
            sp.dma_start(adj_in[1][:, :, :], adj_g[1]).then_inc(d_adj[1], 16)
            load_w(3)
            sp.wait_ge(dve_wlo, 4)
            load_w(4)
            sp.wait_ge(dve_wlo, 5)
            load_w(5)

            def step(pair, u, this, after, before, before2):
                slot = u % 2
                if this and after and u == 0:
                    need(sp, pe_t, 3 * (4 * pair + 1))
                    sp.dma_start(x_in[0][:, :, :], x_g[2 * pair + 2]).then_inc(d_x[0], 16)
                    need(sp, pool_mask, 2 * (2 * pair + 1))
                    sp.dma_start(adj_in[0][:, :, :], adj_g[2 * pair + 2]).then_inc(d_adj[0], 16)
                pair_at = pair if isinstance(pair, int) else sp.snap(2 * pair)
                if before2:
                    need(sp, dve_y, 4 * (2 * (pair - 1) + slot + 1))
                if before2 and u == 0:
                    sp.dma_start(x_res[:, :, :], x_g[2 * pair - 1]).then_inc(d_xres, 16)
                if this and u == 1:
                    if isinstance(pair, int) and pair == 0:
                        sp.wait_ge(dve_wlo, 9)
                    sp.dma_start(x_res[:, :, :], x_g[2 * pair if isinstance(pair, int) else pair_at])\
                        .then_inc(d_xres, 16)
                if this and after and u == 0 or this and after and u == 1:
                    if u == 1:
                        need(sp, pe_t, 3 * (4 * pair + 2))
                        sp.dma_start(x_in[1][:, :, :], x_g[2 * pair + 3]).then_inc(d_x[1], 16)
                        need(sp, pool_mask, 2 * (2 * pair + 2))
                        sp.dma_start(adj_in[1][:, :, :], adj_g[2 * pair + 3]).then_inc(d_adj[1], 16)
                if before2:
                    need(sp, dve_out, 4 * (2 * (pair - 1) + slot + 1))
                    sp.dma_start(out_g[2 * (pair - 1) + slot], y_out[:, :, :]).then_inc(d_out, 16)

            def last_pair(pair, u, this, after, before, before2):
                if isinstance(pair, int) and pair == PAIRS - 1:
                    if u == 0:
                        step(pair, 0, False, False, before, before2)
                    elif u == 1:
                        sp.wait_ge(dve_y, 4 * (2 * (pair - 1) + 2))
                        sp.dma_start(x_res[:, :, :], x_g[2 * pair]).then_inc(d_xres, 16)
                        sp.wait_ge(dve_out, 4 * (2 * (pair - 1) + 2))
                        sp.dma_start(out_g[2 * (pair - 1) + 1], y_out[:, :, :]).then_inc(d_out, 16)
                else:
                    step(pair, u, this, after, before, before2)

            run(sp, last_pair)
            sp.wait_ge(d_out, 16 * 2 * PAIRS)

        @block.tensor
        def _(pe):
            def product3(dst, parts, first, last):
                s_hi, s_lo, m_hi, m_lo = parts
                nc.tensor.matmul(dst, s_hi, m_hi, start=first, stop=False)
                nc.tensor.matmul(dst, s_hi, m_lo, start=False, stop=False)
                return nc.tensor.matmul(dst, s_lo, m_hi, start=False, stop=last)

            def wlin_transposes(l, stage):
                pe.wait_ge(d_w[3 * l], 16)
                for c in range(KC):
                    if l > 0 or c > 0:
                        pe.wait_ge(dve_wlo, 5 * l + c)
                    for o in range(KC):
                        last = nc.tensor.transpose(ps_c[:, o * P:(o + 1) * P],
                                                   stage[:, o, c * P:(c + 1) * P], ident[:, :])
                    last.then_inc(pe_w, 1)

            def step(pair, u, this, after, before, before2):
                k = 4 * pair + u
                layer, hb = u // 2, u % 2
                pb = (u + 1) % 2
                first_unit = isinstance(pair, int) and k == 0

                def values(q):
                    if q == 0:
                        need(pe, dve_tlo, 3 * (k + 1))
                    need(pe, dve_vb, 4 * k + q - 1)
                    for c in range(KC):
                        last = product3(ps_v[q % 2][:, 0:H],
                                        (hT_hi[hb][:, c, q, :], hT_lo[hb][:, c, q, :],
                                         wlin_hi[layer][:, c, :], wlin_lo[layer][:, c, :]),
                                        c == 0, c == KC - 1)
                    last.then_inc(pe_v, 1)

                def projection(o):
                    ch, side = divmod(o, 2)
                    need(pe, dve_nlo, 6 * k + o - 1)
                    for c in range(KC):
                        last = product3(ps_n[o % 2][:, :],
                                        (w_hi[layer][side][:, c, ch * P:(ch + 1) * P],
                                         w_lo[layer][side][:, c, ch * P:(ch + 1) * P],
                                         hT_hi[hb][:, c, :, :], hT_lo[hb][:, c, :, :]),
                                        c == 0, c == KC - 1)
                    last.then_inc(pe_n, 1)

                def scores(q):
                    if q == 0:
                        need(pe, dve_nlo, 6 * (k + 1))
                    if q % 2 == 0:
                        need(pe, dve_um, 2 * (k - 1) + q // 2 + 1)
                    for c in range(KC):
                        last = product3(ps_u[q // 2][:, (q % 2) * 256:(q % 2) * 256 + 256],
                                        (hT_hi[hb][:, c, q, :], hT_lo[hb][:, c, q, :],
                                         n_hi[:, c, q, :, :], n_lo[:, c, q, :, :]),
                                        c == 0, c == KC - 1)
                    if q % 2:
                        last.then_inc(pe_u, 1)

                def context(q):
                    need(pe, pool_elo, 2 * (k - 1) + q // 2 + 1)
                    need(pe, pool_vlo, 4 * (k - 1) + q + 1)
                    need(pe, act_vhi, 4 * (k - 1) + q + 1)
                    need(pe, act_c, 4 * (k - 1) + q)
                    product3(ps_c[:, 0:HV], (e_hi[:, q, :], e_lo[:, q, :], v_hi[pb][:, q, :],
                                             v_lo[pb][:, q, :]), True, True).then_inc(pe_c, 1)

                def transposes(c):
                    if u in (0, 3):
                        tp = pair + (u == 3)
                        src = x_in[pb]
                        if c == 0:
                            need(pe, d_x[pb], 16 * (tp + 1))
                    else:
                        src = c_sb[pb]
                        if c == 0:
                            need(pe, act_norm, 4 * k)
                    if c:
                        if u in (0, 3):
                            need(pe, dve_tlo, 3 * (k + 1) + c)
                        else:
                            need(pe, act_h, 3 * (2 * pair + u - 1) + c)
                    elif u == 0:
                        need(pe, act_at, 2 * pair + 1)
                    elif u == 1:
                        need(pe, act_at, 2 * pair + 2)
                    elif u == 2:
                        need(pe, act_h, 3 * (2 * pair + 1))
                    else:
                        need(pe, act_h, 3 * (2 * pair + 2))
                    for q in range(G):
                        last = nc.tensor.transpose(ps_t[:, q * P:(q + 1) * P],
                                                   src[:, q, c * P:(c + 1) * P], ident[:, :])
                    last.then_inc(pe_t, 1)

                def adj_transposes():
                    if u in (0, 3):
                        tp = pair + (u == 3)
                        need(pe, d_adj[pb], 16 * (tp + 1))
                        need(pe, dve_tlo, 3 * (k + 2))
                        for q in range(G):
                            last = nc.tensor.transpose(ps_t[:, q * P:(q + 1) * P],
                                                       adj_in[pb][:, q, :], ident[:, :])
                        last.then_inc(pe_at, 1)

                if first_unit:
                    pe.wait_ge(dve_wlo, 5)
                if this:
                    values(0)
                    values(1)
                    values(2)
                if before:
                    context(0)
                if this:
                    values(3)
                if before:
                    context(1)
                if this:
                    projection(0)
                if before:
                    context(2)
                if this:
                    projection(1)
                if before:
                    context(3)
                if this:
                    for o in range(2, NO):
                        projection(o)
                if first_unit:
                    wlin_transposes(1, x_res)
                for q in range(G):
                    if after and q < KC:
                        transposes(q)
                    if after and q == KC:
                        adj_transposes()
                    if this:
                        scores(q)

            pe.wait_ge(ident_ready, 1)
            wlin_transposes(0, c_sb[0])
            run(pe, step)

        @block.scalar
        def _(act):
            def split_hi(piece_out, piece_in):
                nc.scalar.activation(piece_out, piece_in, ACT.Copy).then_inc(act_whi, 1)

            def wlin_hi_parts(l):
                for c in range(KC):
                    act.wait_ge(pe_w, KC * l + c + 1)
                    split_hi(wlin_hi[l][:, c, :], ps_c[:, 0:H])

            def w_hi_parts(l, stage):
                for side in range(2):
                    act.wait_ge(d_w[3 * l + 1 + side], 16)
                    split_hi(w_hi[l][side][:, :, :], stage[side])

            def step(pair, u, this, after, before, before2):
                k = 4 * pair + u
                hb, pb = u % 2, (u + 1) % 2
                first_unit = isinstance(pair, int) and k == 0

                def exponent(p):
                    need(act, dve_us, 2 * (k - 1) + p + 1)
                    nc.scalar.activation(ex[:, p], ex[:, p], ACT.Exp, scale=SCALE).then_inc(act_exp, 1)

                def e_high(p):
                    need(act, pool_e, 2 * (k - 1) + p + 1)
                    need(act, pe_c, 4 * (k - 2) + 2 * p + 2)
                    nc.scalar.activation(e_hi[:, 2 * p:2 * p + 2, :], ex[:, p], ACT.Copy)\
                        .then_inc(act_ehi, 1)

                def v_high(q):
                    need(act, dve_vb, 4 * k + q + 1)
                    need(act, pe_c, 4 * (k - 2) + q + 1)
                    nc.scalar.activation(v_hi[hb][:, q, 0:H], vb[:, q % 2, :], ACT.Copy)\
                        .then_inc(act_vhi, 1)

                def c_copy(q):
                    need(act, pe_c, 4 * (k - 1) + q + 1)
                    if u in (0, 3):
                        pass
                    nc.scalar.activation(c_sb[pb][:, q, :], ps_c[:, 0:HV], ACT.Copy).then_inc(act_c, 1)

                def n_high(o):
                    ch, side = divmod(o, 2)
                    need(act, pe_n, 6 * k + o + 1)
                    need(act, pe_u, 2 * k)
                    nc.scalar.activation(n_hi[:, ch, :, side, :],
                                         ps_n[o % 2][:, :].rearrange("p (q i) -> p q i", q=G),
                                         ACT.Copy).then_inc(act_nhi, 1)

                def normalize(q):
                    if q == 0:
                        need(act, dve_shift, k)
                    nc.scalar.activation(c_sb[pb][:, q, 0:H], c_sb[pb][:, q, 0:H], ACT.Identity,
                                         bias=shift[:, q:q + 1], scale=gain[:, q:q + 1])\
                        .then_inc(act_norm, 1)

                def h_high(c):
                    need(act, pe_t, 3 * (k + 1) + c + 1)
                    hi = hT_hi[pb][:, c, :, :]
                    if u in (0, 3):
                        nc.scalar.activation(hi, ps_t[:, :].rearrange("p (q i) -> p q i", q=G), ACT.Copy)\
                            .then_inc(act_thi, 1)
                        return
                    n = 3 * (2 * pair + u - 1) + c + 1
                    need(act, dve_tlo, 3 * (k + 1) + c - 1)
                    nc.scalar.activation(h_full[:, c % 2, :], ps_t[:, :], ACT.Relu,
                                         bias=b0_col[:, c:c + 1], scale=a0_col[:, c:c + 1])\
                        .then_inc(act_h, 1)
                    need(act, act_h, n)
                    nc.scalar.activation(hi, h_full[:, c % 2, :].rearrange("p (q i) -> p q i", q=G),
                                         ACT.Copy).then_inc(act_thi, 1)

                def adj_copy():
                    if u in (0, 3):
                        tp = pair + (u == 3)
                        need(act, pe_at, 2 * tp + pb + 1)
                        need(act, pool_e, 2 * k)
                        nc.scalar.activation(adjT[pb][:, :, :],
                                             ps_t[:, :].rearrange("p (q i) -> p q i", q=G), ACT.Copy)\
                            .then_inc(act_at, 1)

                if before:
                    exponent(0)
                if this:
                    v_high(0)
                if before:
                    e_high(0)
                    exponent(1)
                if this:
                    v_high(1)
                if before:
                    e_high(1)
                if this:
                    v_high(2)
                if before:
                    c_copy(0)
                if this:
                    v_high(3)
                if before:
                    c_copy(1)
                if this:
                    n_high(0)
                if before:
                    c_copy(2)
                if this:
                    n_high(1)
                if before:
                    c_copy(3)
                if this:
                    n_high(2)
                    n_high(3)
                if before:
                    for q in range(G):
                        normalize(q)
                if this:
                    n_high(4)
                    n_high(5)
                if first_unit:
                    wlin_hi_parts(1)
                    w_hi_parts(1, [c_sb[1][:, 0:KC, 0:H], y_out[:, 0:KC, :]])
                if after:
                    for c in range(KC):
                        h_high(c)
                    adj_copy()

            act.wait_ge(d_small, 16 * 5)
            wlin_hi_parts(0)
            w_hi_parts(0, [c_sb[1][:, 0:KC, 0:H], y_out[:, 0:KC, :]])
            run(act, step)

        @block.vector
        def _(dve):
            def split_lo(n, piece_out, whole, piece_hi):
                dve.wait_ge(act_whi, n)
                nc.vector.tensor_tensor(piece_out, whole, piece_hi.bitcast(F32), ALU.subtract)\
                    .then_inc(dve_wlo, 1)

            def weight_lo_parts(l, stage):
                for c in range(KC):
                    split_lo(5 * l + c + 1, wlin_lo[l][:, c, :], ps_c[:, 0:H], wlin_hi[l][:, c, :])
                for side in range(2):
                    split_lo(5 * l + 4 + side, w_lo[l][side][:, :, :], stage[side],
                             w_hi[l][side][:, :, :])

            def step(pair, u, this, after, before, before2):
                k = 4 * pair + u
                layer, hb = u // 2, u % 2
                pb = (u + 1) % 2
                first_unit = isinstance(pair, int) and k == 0
                j = 2 * (pair - 1) + u % 2

                def masked(p):
                    need(dve, pe_u, 2 * (k - 1) + p + 1)
                    if p == 0 and u in (1, 2):
                        need(dve, pool_mask, 2 * (2 * pair + u))
                    nc.vector.tensor_tensor(um[:, p].rearrange("p q s i -> p (q s i)"), ps_u[p][:, :],
                                            mask[pb][:, 2 * p:2 * p + 2].rearrange("p q s i -> p (q s i)"),
                                            ALU.mult).then_inc(dve_um, 1)
                    need(dve, dve_um, 2 * (k - 1) + p + 1)
                    need(dve, pool_elo, 2 * (k - 2) + p + 1)
                    nc.vector.tensor_tensor(ex[:, p], um[:, p, :, 0, :], um[:, p, :, 1, :],
                                            ALU.add).then_inc(dve_us, 1)

                def v_bias(q):
                    need(dve, pe_v, 4 * k + q + 1)
                    need(dve, pool_vlo, 4 * k + q - 1)
                    need(dve, act_vhi, 4 * k + q - 1)
                    nc.vector.tensor_tensor(vb[:, q % 2, :], ps_v[q % 2][:, 0:H], b_bc[:, layer, :],
                                            ALU.add).then_inc(dve_vb, 1)

                def n_low(o):
                    ch, side = divmod(o, 2)
                    need(dve, act_nhi, 6 * k + o + 1)
                    nc.vector.tensor_tensor(n_lo[:, ch, :, side, :],
                                            ps_n[o % 2][:, :].rearrange("p (q i) -> p q i", q=G),
                                            n_hi[:, ch, :, side, :].bitcast(F32),
                                            ALU.subtract).then_inc(dve_nlo, 1)

                def stats(q):
                    need(dve, act_c, 4 * (k - 1) + q + 1)
                    nc.vector.bn_stats(bn[:, q, :], c_sb[pb][:, q, 0:H]).then_inc(dve_bn, 1)

                def aggregate():
                    need(dve, dve_bn, 4 * k)
                    need(dve, dve_den2, k - 1)
                    nc.vector.tensor_scalar(den[:, :], c_sb[pb][:, :, H], 1e-10, 1e-3, ALU.add, ALU.mult)\
                        .then_inc(dve_den, 1)
                    for q in range(G):
                        nc.vector.bn_aggr(mv[:, q, :], bn[:, q, :]).then_inc(dve_mv, 1)

                def layernorm_scalars():
                    need(dve, pool_std, k)
                    need(dve, dve_den, k)
                    nc.vector.scalar_tensor_tensor(den2[:, :], std[:, :], BESSEL, den[:, :],
                                                   ALU.mult, ALU.add).then_inc(dve_den2, 1)
                    need(dve, dve_den2, k)
                    need(dve, act_norm, 4 * (k - 1))
                    nc.vector.reciprocal(gain[:, :], den2[:, :]).then_inc(dve_gain, 1)
                    need(dve, dve_gain, k)
                    nc.vector.scalar_tensor_tensor(shift[:, :], mv[:, :, 0], -1.0, gain[:, :],
                                                   ALU.mult, ALU.mult).then_inc(dve_shift, 1)

                def residual(q):
                    if q == 0:
                        need(dve, d_xres, 16 * (j + 1))
                    need(dve, pool_z, 4 * j + q + 1)
                    nc.vector.scalar_tensor_tensor(c_sb[hb][:, q, 0:H], c_sb[hb][:, q, 0:H], 0.0,
                                                   x_res[:, q, :], ALU.max, ALU.add).then_inc(dve_y, 1)
                    need(dve, dve_y, 4 * j + q + 1)
                    nc.vector.bn_stats(fbn[:, q, :], c_sb[hb][:, q, 0:H]).then_inc(dve_fbn, 1)

                def final_scalars():
                    for q in range(G):
                        nc.vector.bn_aggr(fmv[:, q, :], fbn[:, q, :]).then_inc(dve_fmv, 1)
                    need(dve, dve_fmv, 4 * (j + 1))
                    nc.vector.tensor_scalar(fvar[:, :], fmv[:, :, 1], 1e-5, None, ALU.add)\
                        .then_inc(dve_fvar, 1)

                def final_apply(q):
                    if q == 0:
                        need(dve, pool_rstd, j + 1)
                        need(dve, d_out, 16 * j)
                    nc.vector.tensor_scalar(y_out[:, q, :], c_sb[hb][:, q, 0:H], fmv[:, q, 0:1],
                                            rstd[:, q:q + 1], ALU.subtract, ALU.mult)\
                        .then_inc(dve_out, 1)

                def h_low(c):
                    need(dve, act_thi, 3 * (k + 1) + c + 1)
                    src = ps_t[:, :] if u in (0, 3) else h_full[:, c % 2, :]
                    nc.vector.tensor_tensor(hT_lo[pb][:, c, :, :], src.rearrange("p (q i) -> p q i", q=G),
                                            hT_hi[pb][:, c, :, :].bitcast(F32),
                                            ALU.subtract).then_inc(dve_tlo, 1)

                if before:
                    masked(0)
                if this:
                    v_bias(0)
                if before:
                    masked(1)
                if this:
                    for q in range(1, G):
                        v_bias(q)
                if before:
                    stats(0)
                if this:
                    n_low(0)
                if before:
                    stats(1)
                    stats(2)
                if this:
                    n_low(1)
                if before:
                    stats(3)
                    aggregate()
                if this:
                    n_low(2)
                if before:
                    layernorm_scalars()
                if before2:
                    residual(0)
                if this:
                    n_low(3)
                if before2:
                    residual(1)
                    residual(2)
                if this:
                    n_low(4)
                if before2:
                    residual(3)
                    need(dve, dve_fbn, 4 * (j + 1))
                if this:
                    n_low(5)
                if before2:
                    final_scalars()
                    final_apply(0)
                    final_apply(1)
                if first_unit:
                    weight_lo_parts(1, [c_sb[1][:, 0:KC, 0:H], y_out[:, 0:KC, :]])
                for c in range(KC):
                    if after:
                        h_low(c)
                if before2:
                    final_apply(2)
                    final_apply(3)

            nc.vector.memset(half[:, :], 0.5)
            nc.vector.memset(mhalf[:, :], -0.5)
            for i in range(2):
                nc.vector.memset(v_hi[i][:, :, H:HV].bitcast(F32), 1.0)
                last = nc.vector.memset(v_lo[i][:, :, H:HV].bitcast(F32), 0.0)
            last.then_inc(dve_const, 1)
            dve.wait_ge(d_small, 16 * 5)
            weight_lo_parts(0, [c_sb[1][:, 0:KC, 0:H], y_out[:, 0:KC, :]])
            run(dve, step)

        @block.gpsimd
        def _(pool):
            def step(pair, u, this, after, before, before2):
                k = 4 * pair + u
                hb, pb = u % 2, (u + 1) % 2
                j = 2 * (pair - 1) + u % 2
                i = 2 * pair + (u - 3) if u == 3 else 2 * pair - 1

                def times_adj(p):
                    need(pool, act_exp, 2 * (k - 1) + p + 1)
                    nc.gpsimd.tensor_tensor(ex[:, p], ex[:, p], adjT[pb][:, 2 * p:2 * p + 2, :], ALU.mult)\
                        .then_inc(pool_e, 1)

                def e_low(p):
                    need(pool, act_ehi, 2 * (k - 1) + p + 1)
                    need(pool, pe_c, 4 * (k - 2) + 2 * p + 2)
                    nc.gpsimd.tensor_tensor(e_lo[:, 2 * p:2 * p + 2, :], ex[:, p],
                                            e_hi[:, 2 * p:2 * p + 2, :].bitcast(F32), ALU.subtract)\
                        .then_inc(pool_elo, 1)

                def v_low(q):
                    need(pool, act_vhi, 4 * k + q + 1)
                    nc.gpsimd.tensor_tensor(v_lo[hb][:, q, 0:H], vb[:, q % 2, :],
                                            v_hi[hb][:, q, 0:H].bitcast(F32), ALU.subtract)\
                        .then_inc(pool_vlo, 1)

                if before:
                    times_adj(0)
                if this:
                    v_low(0)
                if before:
                    e_low(0)
                    times_adj(1)
                if this:
                    v_low(1)
                if before:
                    e_low(1)
                if this:
                    v_low(2)
                    v_low(3)
                if before:
                    need(pool, dve_mv, 4 * k)
                    nc.gpsimd.tensor_tensor(std[:, :], mv[:, :, 1], half[:, :], ALU.pow)\
                        .then_inc(pool_std, 1)
                if before and u in (0, 3):
                    for q in range(G):
                        need(pool, act_norm, 4 * (k - 1) + q + 1)
                        z = c_sb[pb][:, q, 0:H]
                        nc.gpsimd.tensor_tensor(z, z, a1_bc[:, :], ALU.mult).then_inc(pool_za, 1)
                        need(pool, pool_za, 4 * i + q + 1)
                        nc.gpsimd.tensor_tensor(z, z, b1_bc[:, :], ALU.add).then_inc(pool_z, 1)
                        if q == 0 and before2:
                            rstd_of(j)
                elif before2:
                    rstd_of(j)
                if after and u in (0, 3):
                    tp = pair + (u == 3)
                    need(pool, act_at, 2 * tp + pb + 1)
                    need(pool, dve_um, 2 * k)
                    for side, a in enumerate((adjT[pb], adj_in[pb])):
                        tri = side_of[:, side:side + 1, :].to_broadcast([P, G, P])
                        nc.gpsimd.tensor_tensor(mask[pb][:, :, side, :], a[:, :, :], tri, ALU.mult)\
                            .then_inc(pool_mask, 1)

            def rstd_of(j):
                need(pool, dve_fvar, j + 1)
                nc.gpsimd.tensor_tensor(rstd[:, :], fvar[:, :], mhalf[:, :], ALU.pow).then_inc(pool_rstd, 1)

            nc.gpsimd.memset(ident[:, :], 0.0).then_inc(ident0, 1)
            pool.wait_ge(ident0, 1)
            nc.gpsimd.affine_select(out=ident[:, :], in_=ident[:, :], compare_op=ALU.not_equal, fill=1.0,
                                    base=0, pattern=[[-1, P]], channel_multiplier=1).then_inc(ident_ready, 1)
            nc.gpsimd.memset(side_of[:, :, :], 1.0).then_inc(ident0, 1)
            pool.wait_ge(ident0, 2)
            nc.gpsimd.affine_select(out=side_of[:, 0, :], in_=side_of[:, 0, :], pattern=[[-1, P]],
                                    compare_op=ALU.is_ge, fill=0.0, base=0, channel_multiplier=1)\
                .then_inc(tri_ready, 1)
            nc.gpsimd.affine_select(out=side_of[:, 1, :], in_=side_of[:, 1, :], pattern=[[1, P]],
                                    compare_op=ALU.is_gt, fill=0.0, base=0, channel_multiplier=-1)\
                .then_inc(tri_ready, 1)
            pool.wait_ge(tri_ready, 2)
            pool.wait_ge(dve_const, 1)
            pool.wait_ge(d_small, 16 * 5)
            run(pool, step)


_INS = ["x", "adj", "L0_gnn_W_left", "L0_gnn_W_right", "L0_gnn_W_lin", "L0_gnn_b_lin", "L0_gnn_ln_a",
        "L0_gnn_ln_b"]


def kernel(**inputs):
    import numpy as _np
    import concourse.bacc as _bacc
    from concourse import mybir as _mybir
    from concourse.bass_utils import run_bass_kernel_spmd as _run

    nc = _bacc.Bacc("TRN2", target_bir_lowering=False, num_devices=1)
    arrays, args = {}, []
    for name in _INS:
        a = _np.ascontiguousarray(inputs[name])
        arrays[f"in_{name}_dram"] = a
        args.append(nc.dram_tensor(f"in_{name}_dram", a.shape, _mybir.dt.from_np(a.dtype),
                                   kind="ExternalInput").ap())
    out_shape = tuple(inputs["x"].shape)
    args.append(nc.dram_tensor("out_0_dram", out_shape, _mybir.dt.float32, kind="ExternalOutput").ap())
    gnn_resnorm_kernel(nc, *args)
    r = _run(nc, [arrays], core_ids=[0])
    return r.results[0]["out_0_dram"]
```

```python
from contextlib import ExitStack
from math import sqrt

import concourse.bass as bass
from concourse import mybir

ALU = mybir.AluOpType
ACT = mybir.ActivationFunctionType
F32 = mybir.dt.float32
F32R = mybir.dt.float32r

P = 128


def gnn_resnorm_kernel(nc, x, adj, w_left, w_right, w_lin, b_lin, ln_a, ln_b, out):
    B, S, H = x.shape
    L = w_left.shape[0]
    G = 4
    KC = H // P
    NO = 2 * KC
    PAIRS = B // G // 2
    HV = H + 2
    assert S == P and L == 2 and B % (2 * G) == 0
    SCALE = 1.0 / sqrt(H)
    BESSEL = sqrt(H / (H - 1))

    x_g = x.rearrange("(g q) s h -> g s q h", q=G)
    adj_g = adj.rearrange("(g q) s t -> g s q t", q=G)
    out_g = out.rearrange("(g q) s h -> g s q h", q=G)

    with ExitStack() as ctx:
        def sb(name, shape, dt=F32):
            return ctx.enter_context(nc.sbuf_tensor(name, shape, dt))

        def sem(name):
            return ctx.enter_context(nc.semaphore(name))

        w_hi = [[sb(f"w{d}{l}_hi", [P, KC, H], F32R) for d in "LR"] for l in range(L)]
        w_lo = [[sb(f"w{d}{l}_lo", [P, KC, H], F32R) for d in "LR"] for l in range(L)]
        wlin_hi = [sb(f"wlinT{l}_hi", [P, KC, H], F32R) for l in range(L)]
        wlin_lo = [sb(f"wlinT{l}_lo", [P, KC, H], F32R) for l in range(L)]
        hT_hi = [sb(f"hT_hi{i}", [P, KC, G, P], F32R) for i in range(2)]
        hT_lo = [sb(f"hT_lo{i}", [P, KC, G, P], F32R) for i in range(2)]
        n_hi = sb("n_hi", [P, KC, G, 2, P], F32R)
        n_lo = sb("n_lo", [P, KC, G, 2, P], F32R)
        v_hi = [sb(f"v_hi{i}", [P, G, HV], F32R) for i in range(2)]
        v_lo = [sb(f"v_lo{i}", [P, G, HV], F32R) for i in range(2)]
        e_hi = sb("e_hi", [P, G, P], F32R)
        e_lo = sb("e_lo", [P, G, P], F32R)
        um = sb("um", [P, 2, 2, 2, P])
        ex = sb("ex", [P, 2, 2, P])
        vb = sb("vb", [P, 2, H])
        h_full = sb("h_full", [P, 2, G * P])
        adjT = [sb(f"adjT{s}", [P, G, P]) for s in range(2)]
        mask = [sb(f"mask{s}", [P, G, 2, P]) for s in range(2)]
        adj_in = [sb(f"adj_in{s}", [P, G, P]) for s in range(2)]
        x_in = [sb(f"x_in{s}", [P, G, H]) for s in range(2)]
        x_res = sb("x_res", [P, G, H])
        c_sb = [sb(f"c_sb{i}", [P, G, HV]) for i in range(2)]
        y_out = sb("y_out", [P, G, H])
        b_bc = sb("b_bc", [P, L, H])
        a1_bc = sb("a1_bc", [P, H])
        b1_bc = sb("b1_bc", [P, H])
        a0_col = sb("a0_col", [P, KC])
        b0_col = sb("b0_col", [P, KC])
        ident = sb("ident", [P, P])
        side_of = sb("side_of", [P, 2, P])
        half = sb("half", [P, G])
        mhalf = sb("mhalf", [P, G])
        bn = sb("bn", [P, G, 6])
        mv = sb("mv", [P, G, 2])
        std = sb("std", [P, G])
        den = sb("den", [P, G])
        den2 = sb("den2", [P, G])
        gain = sb("gain", [P, G])
        shift = sb("shift", [P, G])
        fbn = sb("fbn", [P, G, 6])
        fmv = sb("fmv", [P, G, 2])
        fvar = sb("fvar", [P, G])
        rstd = sb("rstd", [P, G])

        def bank(name):
            return ctx.enter_context(nc.psum_tensor(name, [P, 512], F32))

        ps_v = [bank(f"ps_v{i}") for i in range(2)]
        ps_n = [bank(f"ps_n{i}") for i in range(2)]
        ps_u = [bank(f"ps_u{i}") for i in range(2)]
        ps_c = bank("ps_c")
        ps_t = bank("ps_t")

        t_bank = [ps_t, ps_c, ps_v[1]]
        wlin_bank = [ps_c, ps_v[0], ps_v[1]]

        d_x = [sem(f"d_x{s}") for s in range(2)]
        d_adj = [sem(f"d_adj{s}") for s in range(2)]
        d_xres = sem("d_xres")
        d_out = sem("d_out")
        d_w = [sem(f"d_w{i}") for i in range(3 * L)]
        d_bias = sem("d_bias")
        d_small = sem("d_small")
        ident0 = sem("ident0")
        ident_ready = sem("ident_ready")
        dve_const = sem("dve_const")
        tri_ready = sem("tri_ready")
        pe_w = sem("pe_w")
        act_whi = sem("act_whi")
        dve_wlo = sem("dve_wlo")
        pe_t = sem("pe_t")
        pe_at = sem("pe_at")
        pe_v = sem("pe_v")
        pe_n = sem("pe_n")
        pe_u = sem("pe_u")
        pe_c = sem("pe_c")
        act_h = sem("act_h")
        act_thi = sem("act_thi")
        act_at = sem("act_at")
        act_vhi = sem("act_vhi")
        act_nhi = sem("act_nhi")
        act_exp = sem("act_exp")
        act_ehi = sem("act_ehi")
        act_c = sem("act_c")
        act_norm = sem("act_norm")
        dve_tlo = sem("dve_tlo")
        dve_vb = sem("dve_vb")
        dve_nlo = sem("dve_nlo")
        dve_um = sem("dve_um")
        dve_us = sem("dve_us")
        dve_bn = sem("dve_bn")
        dve_mv = sem("dve_mv")
        dve_den = sem("dve_den")
        dve_den2 = sem("dve_den2")
        dve_gain = sem("dve_gain")
        dve_shift = sem("dve_shift")
        dve_y = sem("dve_y")
        dve_fbn = sem("dve_fbn")
        dve_fmv = sem("dve_fmv")
        dve_fvar = sem("dve_fvar")
        dve_out = sem("dve_out")
        pool_vlo = sem("pool_vlo")
        pool_e = sem("pool_e")
        pool_elo = sem("pool_elo")
        pool_std = sem("pool_std")
        pool_rstd = sem("pool_rstd")
        pool_za = sem("pool_za")
        pool_z = sem("pool_z")
        pool_mask = sem("pool_mask")

        def need(eng, s, n):
            if not isinstance(n, int) or n > 0:
                eng.wait_ge(s, n)

        def run(eng, step):
            step(-1, 3, False, True, False, False)
            for u in range(4):
                step(0, u, True, True, u > 0, False)
            with eng.Fori(1, PAIRS - 1) as pair:
                for u in range(4):
                    step(pair, u, True, True, True, u < 2)
            for u in range(4):
                step(PAIRS - 1, u, True, u < 3, True, u < 2)
            step(PAIRS, 0, False, False, True, True)
            step(PAIRS, 1, False, False, False, True)

        block = ctx.enter_context(nc.Block())

        @block.sync
        def _(sp):
            w_src = [w_lin[0], w_left[0], w_right[0], w_lin[1], w_left[1], w_right[1]]
            stage = [c_sb[0][:, 0:3, 0:H], c_sb[1][:, 0:3, 0:H], y_out[:, 0:3, :], x_res[:, 0:3, :],
                     c_sb[1][:, 0:3, 0:H], y_out[:, 0:3, :]]

            def load_w(i):
                sp.dma_start(stage[i], w_src[i].rearrange("(c p) h -> p c h", p=P)).then_inc(d_w[i], 16)

            sp.dma_start(x_in[0][:, :, :], x_g[0]).then_inc(d_x[0], 16)
            load_w(0)
            sp.dma_start(adj_in[0][:, :, :], adj_g[0]).then_inc(d_adj[0], 16)
            sp.dma_start(b_bc[:, :, :], b_lin.rearrange("(o l) h -> o l h", o=1).to_broadcast([P, L, H]))\
                .then_inc(d_bias, 16)
            load_w(1)
            load_w(2)
            sp.dma_start(x_in[1][:, :, :], x_g[1]).then_inc(d_x[1], 16)
            load_w(3)
            sp.dma_start(adj_in[1][:, :, :], adj_g[1]).then_inc(d_adj[1], 16)
            with nc.allow_non_contiguous_dma(reason="384 words, once"):
                sp.dma_start(a0_col[:, :], ln_a[0].rearrange("(c p) -> p c", p=P)).then_inc(d_small, 16)
                sp.dma_start(b0_col[:, :], ln_b[0].rearrange("(c p) -> p c", p=P)).then_inc(d_small, 16)
            sp.dma_start(a1_bc[:, :], ln_a[1:2].to_broadcast([P, H])).then_inc(d_small, 16)
            sp.dma_start(b1_bc[:, :], ln_b[1:2].to_broadcast([P, H])).then_inc(d_small, 16)
            sp.wait_ge(dve_wlo, 4)
            load_w(4)
            sp.wait_ge(dve_wlo, 5)
            load_w(5)

            def step(pair, u, this, after, before, before2):
                slot = u % 2
                if this and after and u == 0:
                    need(sp, pe_t, 3 * (4 * pair + 1))
                    sp.dma_start(x_in[0][:, :, :], x_g[2 * pair + 2]).then_inc(d_x[0], 16)
                    need(sp, pool_mask, 2 * (2 * pair + 1))
                    sp.dma_start(adj_in[0][:, :, :], adj_g[2 * pair + 2]).then_inc(d_adj[0], 16)
                pair_at = pair if isinstance(pair, int) else sp.snap(2 * pair)
                if before2:
                    need(sp, dve_y, 4 * (2 * (pair - 1) + slot + 1))
                if before2 and u == 0:
                    sp.dma_start(x_res[:, :, :], x_g[2 * pair - 1]).then_inc(d_xres, 16)
                if this and u == 1:
                    if isinstance(pair, int) and pair == 0:
                        sp.wait_ge(dve_wlo, 9)
                    sp.dma_start(x_res[:, :, :], x_g[2 * pair if isinstance(pair, int) else pair_at])\
                        .then_inc(d_xres, 16)
                if this and after and u == 0 or this and after and u == 1:
                    if u == 1:
                        need(sp, pe_t, 3 * (4 * pair + 2))
                        sp.dma_start(x_in[1][:, :, :], x_g[2 * pair + 3]).then_inc(d_x[1], 16)
                        need(sp, pool_mask, 2 * (2 * pair + 2))
                        sp.dma_start(adj_in[1][:, :, :], adj_g[2 * pair + 3]).then_inc(d_adj[1], 16)
                if before2:
                    need(sp, dve_out, 4 * (2 * (pair - 1) + slot + 1))
                    sp.dma_start(out_g[2 * (pair - 1) + slot], y_out[:, :, :]).then_inc(d_out, 16)

            def last_pair(pair, u, this, after, before, before2):
                if isinstance(pair, int) and pair == PAIRS - 1:
                    if u == 0:
                        step(pair, 0, False, False, before, before2)
                    elif u == 1:
                        sp.wait_ge(dve_y, 4 * (2 * (pair - 1) + 2))
                        sp.dma_start(x_res[:, :, :], x_g[2 * pair]).then_inc(d_xres, 16)
                        sp.wait_ge(dve_out, 4 * (2 * (pair - 1) + 2))
                        sp.dma_start(out_g[2 * (pair - 1) + 1], y_out[:, :, :]).then_inc(d_out, 16)
                else:
                    step(pair, u, this, after, before, before2)

            run(sp, last_pair)
            sp.wait_ge(d_out, 16 * 2 * PAIRS)

        @block.tensor
        def _(pe):
            def product3(dst, parts, first, last):
                s_hi, s_lo, m_hi, m_lo = parts
                nc.tensor.matmul(dst, s_hi, m_hi, start=first, stop=False)
                nc.tensor.matmul(dst, s_hi, m_lo, start=False, stop=False)
                return nc.tensor.matmul(dst, s_lo, m_hi, start=False, stop=last)

            def wlin_transposes(l, stage):
                pe.wait_ge(d_w[3 * l], 16)
                for c in range(KC):
                    if l == 0 and c == 0:
                        pe.wait_ge(dve_tlo, 3)
                    if l == 1 and c == 0:
                        pe.wait_ge(dve_vb, 4)
                    for o in range(KC):
                        last = nc.tensor.transpose(wlin_bank[c][:, o * P:(o + 1) * P],
                                                   stage[:, o, c * P:(c + 1) * P], ident[:, :])
                    last.then_inc(pe_w, 1)

            def step(pair, u, this, after, before, before2):
                k = 4 * pair + u
                layer, hb = u // 2, u % 2
                pb = (u + 1) % 2
                first_unit = isinstance(pair, int) and k == 0

                def values(q):
                    if q == 0:
                        need(pe, dve_tlo, 3 * (k + 1))
                    need(pe, dve_vb, 4 * k + q - 1)
                    for c in range(KC):
                        last = product3(ps_v[q % 2][:, 0:H],
                                        (hT_hi[hb][:, c, q, :], hT_lo[hb][:, c, q, :],
                                         wlin_hi[layer][:, c, :], wlin_lo[layer][:, c, :]),
                                        c == 0, c == KC - 1)
                    last.then_inc(pe_v, 1)

                def projection(o):
                    ch, side = divmod(o, 2)
                    if first_unit and o < 2:
                        pe.wait_ge(dve_wlo, 4 + side)
                    need(pe, dve_nlo, 6 * k + o - 1)
                    for c in range(KC):
                        last = product3(ps_n[o % 2][:, :],
                                        (w_hi[layer][side][:, c, ch * P:(ch + 1) * P],
                                         w_lo[layer][side][:, c, ch * P:(ch + 1) * P],
                                         hT_hi[hb][:, c, :, :], hT_lo[hb][:, c, :, :]),
                                        c == 0, c == KC - 1)
                    last.then_inc(pe_n, 1)

                def scores(q, chunks):
                    need(pe, dve_nlo, 6 * k + 2 * chunks[-1] + 2)
                    if q % 2 == 0 and chunks[0] == 0:
                        need(pe, dve_um, 2 * (k - 1) + q // 2 + 1)
                    for c in chunks:
                        last = product3(ps_u[q // 2][:, (q % 2) * 256:(q % 2) * 256 + 256],
                                        (hT_hi[hb][:, c, q, :], hT_lo[hb][:, c, q, :],
                                         n_hi[:, c, q, :, :], n_lo[:, c, q, :, :]),
                                        c == 0, c == KC - 1)
                    if q % 2 and chunks[-1] == KC - 1:
                        last.then_inc(pe_u, 1)

                def context(q):
                    need(pe, pool_elo, 2 * (k - 1) + q // 2 + 1)
                    need(pe, pool_vlo, 4 * (k - 1) + q + 1)
                    need(pe, act_vhi, 4 * (k - 1) + q + 1)
                    need(pe, act_c, 4 * (k - 1) + q)
                    product3(ps_c[:, 0:HV], (e_hi[:, q, :], e_lo[:, q, :], v_hi[pb][:, q, :],
                                             v_lo[pb][:, q, :]), True, True).then_inc(pe_c, 1)

                def transposes(c):
                    if u in (0, 3):
                        tp = pair + (u == 3)
                        src = x_in[pb]
                        if c == 0:
                            need(pe, d_x[pb], 16 * (tp + 1))
                    else:
                        src = c_sb[pb]
                    if c == 0 and this and u < 2:
                        need(pe, act_at, 2 * pair + u + 1)
                    if c == 1:
                        need(pe, act_c, 4 * k)
                        if first_unit:
                            pe.wait_ge(dve_wlo, 8)
                    if c == 2:
                        need(pe, dve_vb, 4 * (k + 1))
                    for q in range(G):
                        if c == 0 and u in (1, 2):
                            need(pe, act_norm, 4 * (k - 1) + q + 1)
                        last = nc.tensor.transpose(t_bank[c][:, q * P:(q + 1) * P],
                                                   src[:, q, c * P:(c + 1) * P], ident[:, :])
                    last.then_inc(pe_t, 1)

                def adj_transposes():
                    if u in (0, 3):
                        tp = pair + (u == 3)
                        need(pe, d_adj[pb], 16 * (tp + 1))
                        need(pe, dve_tlo, 3 * (k + 1) + 1)
                        for q in range(G):
                            last = nc.tensor.transpose(ps_t[:, q * P:(q + 1) * P],
                                                       adj_in[pb][:, q, :], ident[:, :])
                        last.then_inc(pe_at, 1)

                if first_unit:
                    wlin_transposes(0, c_sb[0])
                    pe.wait_ge(dve_wlo, 3)
                if this:
                    values(0)
                    values(1)
                    values(2)
                    projection(0)
                if before:
                    context(0)
                if this:
                    values(3)
                for q in range(1, G):
                    if before:
                        context(q)
                    if this:
                        projection(q)
                if this:
                    projection(4)
                    projection(5)
                if first_unit:
                    wlin_transposes(1, x_res)
                if this:
                    scores(0, (0, 1))
                    scores(2, (0, 1))
                if after:
                    transposes(0)
                    transposes(1)
                    transposes(2)
                if this:
                    scores(0, (2,))
                    scores(2, (2,))
                    scores(1, (0, 1, 2))
                if after:
                    adj_transposes()
                if this:
                    scores(3, (0, 1, 2))

            pe.wait_ge(ident_ready, 1)
            run(pe, step)

        @block.scalar
        def _(act):
            def split_hi(piece_out, piece_in):
                nc.scalar.activation(piece_out, piece_in, ACT.Copy).then_inc(act_whi, 1)

            def wlin_hi_parts(l):
                for c in range(KC):
                    act.wait_ge(pe_w, KC * l + c + 1)
                    split_hi(wlin_hi[l][:, c, :], wlin_bank[c][:, 0:H])

            def w_hi_parts(l, stage):
                for side in range(2):
                    act.wait_ge(d_w[3 * l + 1 + side], 16)
                    split_hi(w_hi[l][side][:, :, :], stage[side])

            def step(pair, u, this, after, before, before2):
                k = 4 * pair + u
                hb, pb = u % 2, (u + 1) % 2
                first_unit = isinstance(pair, int) and k == 0

                def exponent(p):
                    need(act, dve_us, 2 * (k - 1) + p + 1)
                    nc.scalar.activation(ex[:, p], ex[:, p], ACT.Exp, scale=SCALE).then_inc(act_exp, 1)

                def e_high(p):
                    need(act, pool_e, 2 * (k - 1) + p + 1)
                    need(act, pe_c, 4 * (k - 2) + 2 * p + 2)
                    nc.scalar.activation(e_hi[:, 2 * p:2 * p + 2, :], ex[:, p], ACT.Copy)\
                        .then_inc(act_ehi, 1)

                def v_high(q):
                    need(act, dve_vb, 4 * k + q + 1)
                    need(act, pe_c, 4 * (k - 2) + q + 1)
                    nc.scalar.activation(v_hi[hb][:, q, 0:H], vb[:, q % 2, :], ACT.Copy)\
                        .then_inc(act_vhi, 1)

                def c_copy(q):
                    need(act, pe_c, 4 * (k - 1) + q + 1)
                    nc.scalar.activation(c_sb[pb][:, q, :], ps_c[:, 0:HV], ACT.Copy).then_inc(act_c, 1)

                def n_high(o):
                    ch, side = divmod(o, 2)
                    need(act, pe_n, 6 * k + o + 1)
                    need(act, pe_u, 2 * k)
                    nc.scalar.activation(n_hi[:, ch, :, side, :],
                                         ps_n[o % 2][:, :].rearrange("p (q i) -> p q i", q=G),
                                         ACT.Copy).then_inc(act_nhi, 1)

                def normalize(q):
                    if q == 0:
                        need(act, dve_shift, k)
                    nc.scalar.activation(c_sb[pb][:, q, 0:H], c_sb[pb][:, q, 0:H], ACT.Identity,
                                         bias=shift[:, q:q + 1], scale=gain[:, q:q + 1])\
                        .then_inc(act_norm, 1)

                def h_high(c):
                    need(act, pe_t, 3 * (k + 1) + c + 1)
                    hi = hT_hi[pb][:, c, :, :]
                    if u in (0, 3):
                        nc.scalar.activation(hi, t_bank[c][:, :].rearrange("p (q i) -> p q i", q=G), ACT.Copy)\
                            .then_inc(act_thi, 1)
                        return
                    n = 3 * (2 * pair + u - 1) + c + 1
                    if isinstance(pair, int) and k == 1 and c == 0:
                        act.wait_ge(d_small, 16 * 4)
                    need(act, dve_tlo, 3 * (k + 1) + c - 1)
                    nc.scalar.activation(h_full[:, c % 2, :], t_bank[c][:, :], ACT.Relu,
                                         bias=b0_col[:, c:c + 1], scale=a0_col[:, c:c + 1])\
                        .then_inc(act_h, 1)
                    need(act, act_h, n)
                    nc.scalar.activation(hi, h_full[:, c % 2, :].rearrange("p (q i) -> p q i", q=G),
                                         ACT.Copy).then_inc(act_thi, 1)

                def adj_copy():
                    if u in (0, 3):
                        tp = pair + (u == 3)
                        need(act, pe_at, 2 * tp + pb + 1)
                        need(act, pool_e, 2 * k)
                        nc.scalar.activation(adjT[pb][:, :, :],
                                             ps_t[:, :].rearrange("p (q i) -> p q i", q=G), ACT.Copy)\
                            .then_inc(act_at, 1)

                if first_unit:
                    wlin_hi_parts(0)
                    w_hi_parts(0, [c_sb[1][:, 0:KC, 0:H], y_out[:, 0:KC, :]])
                if before:
                    exponent(0)
                if this:
                    v_high(0)
                if before:
                    e_high(0)
                    exponent(1)
                if this:
                    v_high(1)
                if before:
                    e_high(1)
                if this:
                    v_high(2)
                    n_high(0)
                if before:
                    c_copy(0)
                if this:
                    v_high(3)
                for q in range(1, G):
                    if before:
                        c_copy(q)
                    if this:
                        n_high(q)
                if before:
                    normalize(0)
                    normalize(1)
                if this:
                    n_high(4)
                if before:
                    normalize(2)
                if this:
                    n_high(5)
                if before:
                    normalize(3)
                if first_unit:
                    wlin_hi_parts(1)
                    w_hi_parts(1, [c_sb[1][:, 0:KC, 0:H], y_out[:, 0:KC, :]])
                if after:
                    for c in range(KC):
                        h_high(c)
                    adj_copy()

            run(act, step)

        @block.vector
        def _(dve):
            def split_lo(n, piece_out, whole, piece_hi):
                dve.wait_ge(act_whi, n)
                nc.vector.tensor_tensor(piece_out, whole, piece_hi.bitcast(F32), ALU.subtract)\
                    .then_inc(dve_wlo, 1)

            def weight_lo_parts(l, stage):
                for c in range(KC):
                    split_lo(5 * l + c + 1, wlin_lo[l][:, c, :], wlin_bank[c][:, 0:H], wlin_hi[l][:, c, :])
                for side in range(2):
                    split_lo(5 * l + 4 + side, w_lo[l][side][:, :, :], stage[side],
                             w_hi[l][side][:, :, :])

            def step(pair, u, this, after, before, before2):
                k = 4 * pair + u
                layer, hb = u // 2, u % 2
                pb = (u + 1) % 2
                first_unit = isinstance(pair, int) and k == 0
                j = 2 * (pair - 1) + u % 2

                def masked(p):
                    need(dve, pe_u, 2 * (k - 1) + p + 1)
                    if p == 0 and u in (1, 2):
                        need(dve, pool_mask, 2 * (2 * pair + u))
                    nc.vector.tensor_tensor(um[:, p].rearrange("p q s i -> p (q s i)"), ps_u[p][:, :],
                                            mask[pb][:, 2 * p:2 * p + 2].rearrange("p q s i -> p (q s i)"),
                                            ALU.mult).then_inc(dve_um, 1)
                    need(dve, dve_um, 2 * (k - 1) + p + 1)
                    need(dve, pool_elo, 2 * (k - 2) + p + 1)
                    nc.vector.tensor_tensor(ex[:, p], um[:, p, :, 0, :], um[:, p, :, 1, :],
                                            ALU.add).then_inc(dve_us, 1)

                def v_bias(q):
                    need(dve, pe_v, 4 * k + q + 1)
                    need(dve, pool_vlo, 4 * k + q - 1)
                    need(dve, act_vhi, 4 * k + q - 1)
                    nc.vector.tensor_tensor(vb[:, q % 2, :], ps_v[q % 2][:, 0:H], b_bc[:, layer, :],
                                            ALU.add).then_inc(dve_vb, 1)

                def n_low(o):
                    ch, side = divmod(o, 2)
                    need(dve, act_nhi, 6 * k + o + 1)
                    nc.vector.tensor_tensor(n_lo[:, ch, :, side, :],
                                            ps_n[o % 2][:, :].rearrange("p (q i) -> p q i", q=G),
                                            n_hi[:, ch, :, side, :].bitcast(F32),
                                            ALU.subtract).then_inc(dve_nlo, 1)

                def stats(q):
                    need(dve, act_c, 4 * (k - 1) + q + 1)
                    nc.vector.bn_stats(bn[:, q, :], c_sb[pb][:, q, 0:H]).then_inc(dve_bn, 1)

                def aggregate():
                    need(dve, dve_bn, 4 * k)
                    need(dve, dve_den2, k - 1)
                    nc.vector.tensor_scalar(den[:, :], c_sb[pb][:, :, H], 1e-10, 1e-3, ALU.add, ALU.mult)\
                        .then_inc(dve_den, 1)
                    for q in range(G):
                        nc.vector.bn_aggr(mv[:, q, :], bn[:, q, :]).then_inc(dve_mv, 1)

                def layernorm_scalars():
                    need(dve, pool_std, k)
                    need(dve, dve_den, k)
                    nc.vector.scalar_tensor_tensor(den2[:, :], std[:, :], BESSEL, den[:, :],
                                                   ALU.mult, ALU.add).then_inc(dve_den2, 1)
                    need(dve, dve_den2, k)
                    need(dve, act_norm, 4 * (k - 1))
                    nc.vector.reciprocal(gain[:, :], den2[:, :]).then_inc(dve_gain, 1)
                    need(dve, dve_gain, k)
                    nc.vector.scalar_tensor_tensor(shift[:, :], mv[:, :, 0], -1.0, gain[:, :],
                                                   ALU.mult, ALU.mult).then_inc(dve_shift, 1)

                def residual(q):
                    if q == 0:
                        need(dve, d_xres, 16 * (j + 1))
                    need(dve, pool_z, 4 * j + q + 1)
                    nc.vector.scalar_tensor_tensor(c_sb[hb][:, q, 0:H], c_sb[hb][:, q, 0:H], 0.0,
                                                   x_res[:, q, :], ALU.max, ALU.add).then_inc(dve_y, 1)
                    need(dve, dve_y, 4 * j + q + 1)
                    nc.vector.bn_stats(fbn[:, q, :], c_sb[hb][:, q, 0:H]).then_inc(dve_fbn, 1)

                def final_scalars():
                    for q in range(G):
                        nc.vector.bn_aggr(fmv[:, q, :], fbn[:, q, :]).then_inc(dve_fmv, 1)
                    need(dve, dve_fmv, 4 * (j + 1))
                    nc.vector.tensor_scalar(fvar[:, :], fmv[:, :, 1], 1e-5, None, ALU.add)\
                        .then_inc(dve_fvar, 1)

                def final_apply(q):
                    if q == 0:
                        need(dve, pool_rstd, j + 1)
                        need(dve, d_out, 16 * j)
                    nc.vector.tensor_scalar(y_out[:, q, :], c_sb[hb][:, q, 0:H], fmv[:, q, 0:1],
                                            rstd[:, q:q + 1], ALU.subtract, ALU.mult)\
                        .then_inc(dve_out, 1)

                def h_low(c):
                    need(dve, act_thi, 3 * (k + 1) + c + 1)
                    src = t_bank[c][:, :] if u in (0, 3) else h_full[:, c % 2, :]
                    nc.vector.tensor_tensor(hT_lo[pb][:, c, :, :], src.rearrange("p (q i) -> p q i", q=G),
                                            hT_hi[pb][:, c, :, :].bitcast(F32),
                                            ALU.subtract).then_inc(dve_tlo, 1)

                if first_unit:
                    weight_lo_parts(0, [c_sb[1][:, 0:KC, 0:H], y_out[:, 0:KC, :]])
                if before:
                    masked(0)
                if this:
                    v_bias(0)
                if before:
                    masked(1)
                if this:
                    v_bias(1)
                    v_bias(2)
                    n_low(0)
                if before2:
                    residual(0)
                if before:
                    stats(0)
                if this:
                    v_bias(3)
                if before:
                    stats(1)
                if before2:
                    residual(1)
                if this:
                    n_low(1)
                if before:
                    stats(2)
                if this:
                    n_low(2)
                if before2:
                    residual(2)
                if before:
                    stats(3)
                    aggregate()
                if this:
                    n_low(3)
                if before:
                    layernorm_scalars()
                if before2:
                    residual(3)
                    need(dve, dve_fbn, 4 * (j + 1))
                if this:
                    n_low(4)
                if before2:
                    final_scalars()
                if this:
                    n_low(5)
                if first_unit:
                    weight_lo_parts(1, [c_sb[1][:, 0:KC, 0:H], y_out[:, 0:KC, :]])
                if after:
                    h_low(0)
                    h_low(1)
                if before2:
                    final_apply(0)
                    final_apply(1)
                if after:
                    h_low(2)
                if before2:
                    final_apply(2)
                    final_apply(3)

            nc.vector.memset(half[:, :], 0.5)
            nc.vector.memset(mhalf[:, :], -0.5)
            for i in range(2):
                nc.vector.memset(v_hi[i][:, :, H:HV].bitcast(F32), 1.0)
                last = nc.vector.memset(v_lo[i][:, :, H:HV].bitcast(F32), 0.0)
            last.then_inc(dve_const, 1)
            dve.wait_ge(d_bias, 16)
            run(dve, step)

        @block.gpsimd
        def _(pool):
            def step(pair, u, this, after, before, before2):
                k = 4 * pair + u
                hb, pb = u % 2, (u + 1) % 2
                j = 2 * (pair - 1) + u % 2
                i = 2 * pair + (u - 3) if u == 3 else 2 * pair - 1

                def times_adj(p):
                    need(pool, act_exp, 2 * (k - 1) + p + 1)
                    nc.gpsimd.tensor_tensor(ex[:, p], ex[:, p], adjT[pb][:, 2 * p:2 * p + 2, :], ALU.mult)\
                        .then_inc(pool_e, 1)

                def e_low(p):
                    need(pool, act_ehi, 2 * (k - 1) + p + 1)
                    need(pool, pe_c, 4 * (k - 2) + 2 * p + 2)
                    nc.gpsimd.tensor_tensor(e_lo[:, 2 * p:2 * p + 2, :], ex[:, p],
                                            e_hi[:, 2 * p:2 * p + 2, :].bitcast(F32), ALU.subtract)\
                        .then_inc(pool_elo, 1)

                def v_low(q):
                    need(pool, act_vhi, 4 * k + q + 1)
                    nc.gpsimd.tensor_tensor(v_lo[hb][:, q, 0:H], vb[:, q % 2, :],
                                            v_hi[hb][:, q, 0:H].bitcast(F32), ALU.subtract)\
                        .then_inc(pool_vlo, 1)

                if before:
                    times_adj(0)
                if this:
                    v_low(0)
                if before:
                    e_low(0)
                    times_adj(1)
                if this:
                    v_low(1)
                if before:
                    e_low(1)
                if this:
                    v_low(2)
                    v_low(3)
                if before2:
                    affine(hb, j, k - 2, 2)
                    affine(hb, j, k - 2, 3)
                if before:
                    need(pool, dve_mv, 4 * k)
                    nc.gpsimd.tensor_tensor(std[:, :], mv[:, :, 1], half[:, :], ALU.pow)\
                        .then_inc(pool_std, 1)
                if this and u < 2:
                    need(pool, act_at, 2 * pair + u + 1)
                    need(pool, dve_um, 2 * (k - 1))
                    for side, a in enumerate((adjT[hb], adj_in[hb])):
                        tri = side_of[:, side:side + 1, :].to_broadcast([P, G, P])
                        nc.gpsimd.tensor_tensor(mask[hb][:, :, side, :], a[:, :, :], tri, ALU.mult)\
                            .then_inc(pool_mask, 1)
                if before and u in (0, 3):
                    affine(pb, i, k - 1, 0)
                if before2:
                    need(pool, dve_fvar, j + 1)
                    nc.gpsimd.tensor_tensor(rstd[:, :], fvar[:, :], mhalf[:, :], ALU.pow)\
                        .then_inc(pool_rstd, 1)
                if before and u in (0, 3):
                    affine(pb, i, k - 1, 1)

            def affine(buf, group, unit, q):
                need(pool, act_norm, 4 * unit + q + 1)
                z = c_sb[buf][:, q, 0:H]
                nc.gpsimd.tensor_tensor(z, z, a1_bc[:, :], ALU.mult).then_inc(pool_za, 1)
                need(pool, pool_za, 4 * group + q + 1)
                nc.gpsimd.tensor_tensor(z, z, b1_bc[:, :], ALU.add).then_inc(pool_z, 1)

            nc.gpsimd.memset(ident[:, :], 0.0).then_inc(ident0, 1)
            pool.wait_ge(ident0, 1)
            nc.gpsimd.affine_select(out=ident[:, :], in_=ident[:, :], compare_op=ALU.not_equal, fill=1.0,
                                    base=0, pattern=[[-1, P]], channel_multiplier=1).then_inc(ident_ready, 1)
            nc.gpsimd.memset(side_of[:, :, :], 1.0).then_inc(ident0, 1)
            pool.wait_ge(ident0, 2)
            nc.gpsimd.affine_select(out=side_of[:, 0, :], in_=side_of[:, 0, :], pattern=[[-1, P]],
                                    compare_op=ALU.is_ge, fill=0.0, base=0, channel_multiplier=1)\
                .then_inc(tri_ready, 1)
            nc.gpsimd.affine_select(out=side_of[:, 1, :], in_=side_of[:, 1, :], pattern=[[1, P]],
                                    compare_op=ALU.is_gt, fill=0.0, base=0, channel_multiplier=-1)\
                .then_inc(tri_ready, 1)
            pool.wait_ge(tri_ready, 2)
            pool.wait_ge(dve_const, 1)
            pool.wait_ge(d_small, 16 * 4)
            run(pool, step)


_INS = ["x", "adj", "L0_gnn_W_left", "L0_gnn_W_right", "L0_gnn_W_lin", "L0_gnn_b_lin", "L0_gnn_ln_a",
        "L0_gnn_ln_b"]


def kernel(**inputs):
    import numpy as _np
    import concourse.bacc as _bacc
    from concourse import mybir as _mybir
    from concourse.bass_utils import run_bass_kernel_spmd as _run

    nc = _bacc.Bacc("TRN2", target_bir_lowering=False, num_devices=1)
    arrays, args = {}, []
    for name in _INS:
        a = _np.ascontiguousarray(inputs[name])
        arrays[f"in_{name}_dram"] = a
        args.append(nc.dram_tensor(f"in_{name}_dram", a.shape, _mybir.dt.from_np(a.dtype),
                                   kind="ExternalInput").ap())
    out_shape = tuple(inputs["x"].shape)
    args.append(nc.dram_tensor("out_0_dram", out_shape, _mybir.dt.float32, kind="ExternalOutput").ap())
    gnn_resnorm_kernel(nc, *args)
    r = _run(nc, [arrays], core_ids=[0])
    return r.results[0]["out_0_dram"]
```

```python
from contextlib import ExitStack
from math import sqrt

import concourse.bass as bass
from concourse import mybir

ALU = mybir.AluOpType
ACT = mybir.ActivationFunctionType
F32 = mybir.dt.float32
F32R = mybir.dt.float32r

P = 128


def gnn_resnorm_kernel(nc, x, adj, w_left, w_right, w_lin, b_lin, ln_a, ln_b, out):
    B, S, H = x.shape
    L = w_left.shape[0]
    G = 4
    KC = H // P
    NO = 2 * KC
    PAIRS = B // G // 2
    HV = H + 2
    assert S == P and L == 2 and B % (2 * G) == 0
    SCALE = 1.0 / sqrt(H)
    BESSEL = sqrt(H / (H - 1))

    x_g = x.rearrange("(g q) s h -> g s q h", q=G)
    adj_g = adj.rearrange("(g q) s t -> g s q t", q=G)
    out_g = out.rearrange("(g q) s h -> g s q h", q=G)

    with ExitStack() as ctx:
        def sb(name, shape, dt=F32):
            return ctx.enter_context(nc.sbuf_tensor(name, shape, dt))

        def sem(name):
            return ctx.enter_context(nc.semaphore(name))

        w_hi = [[sb(f"w{d}{l}_hi", [P, KC, H], F32R) for d in "LR"] for l in range(L)]
        w_lo = [[sb(f"w{d}{l}_lo", [P, KC, H], F32R) for d in "LR"] for l in range(L)]
        wlin_hi = [sb(f"wlinT{l}_hi", [P, KC, H], F32R) for l in range(L)]
        wlin_lo = [sb(f"wlinT{l}_lo", [P, KC, H], F32R) for l in range(L)]
        hT_hi = [sb(f"hT_hi{i}", [P, KC, G, P], F32R) for i in range(2)]
        hT_lo = [sb(f"hT_lo{i}", [P, KC, G, P], F32R) for i in range(2)]
        n_hi = sb("n_hi", [P, KC, G, 2, P], F32R)
        n_lo = sb("n_lo", [P, KC, G, 2, P], F32R)
        v_hi = [sb(f"v_hi{i}", [P, G, HV], F32R) for i in range(2)]
        v_lo = [sb(f"v_lo{i}", [P, G, HV], F32R) for i in range(2)]
        e_hi = sb("e_hi", [P, G, P], F32R)
        e_lo = sb("e_lo", [P, G, P], F32R)
        um = sb("um", [P, 2, 2, 2, P])
        ex = sb("ex", [P, 2, 2, P])
        vb = sb("vb", [P, 2, H])
        h_full = sb("h_full", [P, KC, G * P])
        adjT = [sb(f"adjT{s}", [P, G, P]) for s in range(2)]
        mask = [sb(f"mask{s}", [P, G, 2, P]) for s in range(2)]
        adj_in = [sb(f"adj_in{s}", [P, G, P]) for s in range(2)]
        x_in = [sb(f"x_in{s}", [P, G, H]) for s in range(2)]
        x_res = sb("x_res", [P, G, H])
        c_sb = [sb(f"c_sb{i}", [P, G, HV]) for i in range(2)]
        y_out = sb("y_out", [P, G, H])
        b_bc = sb("b_bc", [P, L, H])
        a1_bc = sb("a1_bc", [P, H])
        b1_bc = sb("b1_bc", [P, H])
        a0_col = sb("a0_col", [P, KC])
        b0_col = sb("b0_col", [P, KC])
        ident = sb("ident", [P, P])
        side_of = sb("side_of", [P, 2, P])
        warm = sb("warm", [P, G])
        half = sb("half", [P, G])
        mhalf = sb("mhalf", [P, G])
        bn = sb("bn", [P, G, 6])
        mv = sb("mv", [P, G, 2])
        std = sb("std", [P, G])
        den = sb("den", [P, G])
        den2 = sb("den2", [P, G])
        gain = sb("gain", [P, G])
        shift = sb("shift", [P, G])
        fbn = sb("fbn", [P, G, 6])
        fmv = sb("fmv", [P, G, 2])
        fvar = sb("fvar", [P, G])
        rstd = sb("rstd", [P, G])

        def bank(name):
            return ctx.enter_context(nc.psum_tensor(name, [P, 512], F32))

        ps_v = [bank(f"ps_v{i}") for i in range(2)]
        ps_n = [bank(f"ps_n{i}") for i in range(2)]
        ps_u = [bank(f"ps_u{i}") for i in range(2)]
        ps_c = bank("ps_c")
        ps_t = bank("ps_t")

        t_bank = [ps_t, ps_c, ps_v[1]]
        wlin_bank = [ps_u + [ps_n[0]], [ps_c] + ps_v]

        def c_bank(q, this):
            return ps_c if this or q % 2 == 0 else ps_t

        d_x = [sem(f"d_x{s}") for s in range(2)]
        d_adj = [sem(f"d_adj{s}") for s in range(2)]
        d_xres = sem("d_xres")
        d_out = sem("d_out")
        d_w = [sem(f"d_w{i}") for i in range(3 * L - 1)] + [d_out]
        d_bias = sem("d_bias")
        d_small = sem("d_small")
        pool_fill = sem("pool_fill")
        ident_ready = sem("ident_ready")
        dve_const = sem("dve_const")
        tri_ready = sem("tri_ready")
        pe_w = sem("pe_w")
        act_whi = sem("act_whi")
        dve_wlo = sem("dve_wlo")
        pe_t = sem("pe_t")
        pe_at = sem("pe_at")
        pe_v = sem("pe_v")
        pe_n = sem("pe_n")
        pe_u = sem("pe_u")
        pe_c = sem("pe_c")
        act_h = sem("act_h")
        act_thi = sem("act_thi")
        dve_thi = sem("dve_thi")
        act_at = sem("act_at")
        act_vhi = sem("act_vhi")
        act_nhi = sem("act_nhi")
        act_exp = sem("act_exp")
        act_ehi = sem("act_ehi")
        act_c = sem("act_c")
        act_norm = sem("act_norm")
        dve_norm = sem("dve_norm")
        dve_za = sem("dve_za")
        dve_z = sem("dve_z")
        dve_tlo = sem("dve_tlo")
        dve_vb = sem("dve_vb")
        dve_nlo = sem("dve_nlo")
        dve_um = sem("dve_um")
        dve_us = sem("dve_us")
        dve_bn = sem("dve_bn")
        dve_mv = sem("dve_mv")
        dve_den = sem("dve_den")
        dve_den2 = sem("dve_den2")
        dve_gain = sem("dve_gain")
        dve_shift = sem("dve_shift")
        dve_y = sem("dve_y")
        dve_fbn = sem("dve_fbn")
        dve_fmv = sem("dve_fmv")
        dve_fvar = sem("dve_fvar")
        dve_out = sem("dve_out")
        pool_vlo = sem("pool_vlo")
        pool_e = sem("pool_e")
        pool_elo = sem("pool_elo")
        pool_std = sem("pool_std")
        pool_rstd = sem("pool_rstd")
        pool_za = sem("pool_za")
        pool_z = sem("pool_z")
        pool_mask = sem("pool_mask")

        def need(eng, s, n):
            if not isinstance(n, int) or n > 0:
                eng.wait_ge(s, n)

        def run(eng, step):
            step(-1, 3, False, True, False, False)
            for u in range(4):
                step(0, u, True, True, u > 0, False)
            with eng.Fori(1, PAIRS - 1) as pair:
                for u in range(4):
                    step(pair, u, True, True, True, u < 2)
            for u in range(4):
                step(PAIRS - 1, u, True, u < 3, True, u < 2)
            step(PAIRS, 0, False, False, True, True)
            step(PAIRS, 1, False, False, False, True)

        block = ctx.enter_context(nc.Block())

        @block.sync
        def _(sp):
            w_src = [w_lin[0], w_left[0], w_right[0], w_lin[1], w_left[1], w_right[1]]
            stage = [c_sb[0][:, 0:3, 0:H], c_sb[1][:, 0:3, 0:H], y_out[:, 0:3, :], x_res[:, 0:3, :],
                     c_sb[1][:, 0:3, 0:H], y_out[:, 0:3, :]]

            def load_w(i):
                sp.dma_start(stage[i], w_src[i].rearrange("(c p) h -> p c h", p=P)).then_inc(d_w[i], 16)

            sp.dma_start(x_in[0][:, :, :], x_g[0]).then_inc(d_x[0], 16)
            load_w(0)
            load_w(1)
            sp.dma_start(adj_in[0][:, :, :], adj_g[0]).then_inc(d_adj[0], 16)
            load_w(2)
            sp.dma_start(b_bc[:, :, :], b_lin.rearrange("(o l) h -> o l h", o=1).to_broadcast([P, L, H]))\
                .then_inc(d_bias, 16)
            sp.dma_start(x_in[1][:, :, :], x_g[1]).then_inc(d_x[1], 16)
            load_w(3)
            sp.dma_start(adj_in[1][:, :, :], adj_g[1]).then_inc(d_adj[1], 16)
            with nc.allow_non_contiguous_dma(reason="384 words, once"):
                sp.dma_start(a0_col[:, :], ln_a[0].rearrange("(c p) -> p c", p=P)).then_inc(d_small, 16)
                sp.dma_start(b0_col[:, :], ln_b[0].rearrange("(c p) -> p c", p=P)).then_inc(d_small, 16)
            sp.dma_start(a1_bc[:, :], ln_a[1:2].to_broadcast([P, H])).then_inc(d_small, 16)
            sp.dma_start(b1_bc[:, :], ln_b[1:2].to_broadcast([P, H])).then_inc(d_small, 16)
            sp.wait_ge(dve_wlo, 4)
            load_w(4)
            sp.wait_ge(dve_wlo, 5)
            load_w(5)

            def step(pair, u, this, after, before, before2):
                slot = u % 2
                if this and after and u == 0:
                    need(sp, pe_t, 3 * (4 * pair + 1))
                    sp.dma_start(x_in[0][:, :, :], x_g[2 * pair + 2]).then_inc(d_x[0], 16)
                    need(sp, pool_mask, 2 * (2 * pair + 1))
                    sp.dma_start(adj_in[0][:, :, :], adj_g[2 * pair + 2]).then_inc(d_adj[0], 16)
                this_a = 2 * pair if isinstance(pair, int) else sp.snap(2 * pair)
                if isinstance(pair, int) and pair == PAIRS:
                    this_a = None
                if before2 and this_a is not None:
                    need(sp, dve_y, 4 * (2 * (pair - 1) + slot + 1))
                if before2 and u == 0 and this_a is not None:
                    sp.dma_start(x_res[:, :, :], x_g[2 * pair - 1]).then_inc(d_xres, 16)
                if this and u == 1:
                    if isinstance(pair, int) and pair == 0:
                        sp.wait_ge(dve_wlo, 9)
                    sp.dma_start(x_res[:, :, :], x_g[this_a])\
                        .then_inc(d_xres, 16)
                if this and after and u == 1:
                    need(sp, pe_t, 3 * (4 * pair + 2))
                    sp.dma_start(x_in[1][:, :, :], x_g[2 * pair + 3]).then_inc(d_x[1], 16)
                    need(sp, pool_mask, 2 * (2 * pair + 2))
                    sp.dma_start(adj_in[1][:, :, :], adj_g[2 * pair + 3]).then_inc(d_adj[1], 16)
                if isinstance(pair, int) and 4 * pair + u == 4 * PAIRS + 1:
                    for q in (0, 2):
                        sp.wait_ge(dve_out, 4 * (2 * PAIRS - 1) + q + 2)
                        sp.dma_start(out_g[2 * PAIRS - 1][:, q:q + 2, :], y_out[:, q:q + 2, :])\
                            .then_inc(d_out, 16)
                elif before2:
                    need(sp, dve_out, 4 * (2 * (pair - 1) + slot + 1))
                    sp.dma_start(out_g[2 * (pair - 1) + slot], y_out[:, :, :]).then_inc(d_out, 16)

            def last_pair(pair, u, this, after, before, before2):
                if isinstance(pair, int) and pair == PAIRS - 1:
                    if u == 0:
                        step(pair, 0, False, False, before, before2)
                    elif u == 1:
                        sp.wait_ge(dve_out, 4 * (2 * (pair - 1) + 2))
                        sp.dma_start(out_g[2 * (pair - 1) + 1], y_out[:, :, :]).then_inc(d_out, 16)
                else:
                    step(pair, u, this, after, before, before2)

            run(sp, last_pair)
            sp.wait_ge(d_out, 16 * (2 * PAIRS + 2))

        @block.tensor
        def _(pe):
            def product3(dst, parts, first, last):
                s_hi, s_lo, m_hi, m_lo = parts
                nc.tensor.matmul(dst, s_hi, m_hi, start=first, stop=False)
                nc.tensor.matmul(dst, s_hi, m_lo, start=False, stop=False)
                return nc.tensor.matmul(dst, s_lo, m_hi, start=False, stop=last)

            def wlin_transposes(l, stage):
                pe.wait_ge(d_w[3 * l], 16)
                for c in range(KC):
                    if l == 1 and c == 0:
                        pe.wait_ge(dve_vb, 4)
                    for o in range(KC):
                        last = nc.tensor.transpose(wlin_bank[l][c][:, o * P:(o + 1) * P],
                                                   stage[:, o, c * P:(c + 1) * P], ident[:, :])
                    last.then_inc(pe_w, 1)

            def step(pair, u, this, after, before, before2):
                k = 4 * pair + u
                layer, hb = u // 2, u % 2
                pb = (u + 1) % 2
                first_unit = isinstance(pair, int) and k == 0

                def values(q):
                    need(pe, dve_vb, 4 * k + q - 1)
                    for c in range(KC):
                        if q == 0:
                            need(pe, dve_tlo, 3 * k + c + 1)
                        last = product3(ps_v[q % 2][:, 0:H],
                                        (hT_hi[hb][:, c, q, :], hT_lo[hb][:, c, q, :],
                                         wlin_hi[layer][:, c, :], wlin_lo[layer][:, c, :]),
                                        c == 0, c == KC - 1)
                    last.then_inc(pe_v, 1)

                def projection(o):
                    ch, side = divmod(o, 2)
                    if first_unit and o < 2:
                        pe.wait_ge(dve_wlo, 4 + side)
                    need(pe, dve_nlo, 6 * k + o - 1)
                    for c in range(KC):
                        last = product3(ps_n[o % 2][:, :],
                                        (w_hi[layer][side][:, c, ch * P:(ch + 1) * P],
                                         w_lo[layer][side][:, c, ch * P:(ch + 1) * P],
                                         hT_hi[hb][:, c, :, :], hT_lo[hb][:, c, :, :]),
                                        c == 0, c == KC - 1)
                    last.then_inc(pe_n, 1)

                def scores(q, chunks):
                    need(pe, dve_nlo, 6 * k + 2 * chunks[-1] + 2)
                    if q % 2 == 0 and chunks[0] == 0:
                        need(pe, dve_um, 2 * (k - 1) + q // 2 + 1)
                    for c in chunks:
                        last = product3(ps_u[q // 2][:, (q % 2) * 256:(q % 2) * 256 + 256],
                                        (hT_hi[hb][:, c, q, :], hT_lo[hb][:, c, q, :],
                                         n_hi[:, c, q, :, :], n_lo[:, c, q, :, :]),
                                        c == 0, c == KC - 1)
                    if q % 2 and chunks[-1] == KC - 1:
                        last.then_inc(pe_u, 1)

                def context(q):
                    need(pe, pool_elo, 2 * (k - 1) + q // 2 + 1)
                    need(pe, pool_vlo, 4 * (k - 1) + q + 1)
                    need(pe, act_vhi, 4 * (k - 1) + q + 1)
                    need(pe, act_c, 4 * (k - 1) + q - (not this and q > 0))
                    product3(c_bank(q, this)[:, 0:HV], (e_hi[:, q, :], e_lo[:, q, :], v_hi[pb][:, q, :],
                                             v_lo[pb][:, q, :]), True, True).then_inc(pe_c, 1)

                def transposes(c):
                    if u in (0, 3):
                        tp = pair + (u == 3)
                        src = x_in[pb]
                        if c == 0:
                            need(pe, d_x[pb], 16 * (tp + 1))
                    else:
                        src = c_sb[pb]
                    if c == 0 and this and u < 2:
                        need(pe, act_at, 2 * pair + u + 1)
                    if c == 1:
                        need(pe, act_c, 4 * k)
                        if first_unit:
                            pe.wait_ge(dve_wlo, 8)
                    if c == 2:
                        need(pe, dve_vb, 4 * (k + 1))
                    for q in range(G):
                        if c == 0 and u in (1, 2):
                            if q < 2:
                                need(pe, dve_norm, 2 * (2 * pair + u - 1) + q + 1)
                            else:
                                need(pe, act_norm, 2 * (k - 1) + q - 1)
                        last = nc.tensor.transpose(t_bank[c][:, q * P:(q + 1) * P],
                                                   src[:, q, c * P:(c + 1) * P], ident[:, :])
                    last.then_inc(pe_t, 1)

                def adj_transposes():
                    if u in (0, 3):
                        tp = pair + (u == 3)
                        need(pe, d_adj[pb], 16 * (tp + 1))
                        need(pe, dve_tlo, 3 * (k + 1) + 1)
                        for q in range(G):
                            last = nc.tensor.transpose(ps_t[:, q * P:(q + 1) * P],
                                                       adj_in[pb][:, q, :], ident[:, :])
                        last.then_inc(pe_at, 1)

                if first_unit:
                    pe.wait_ge(dve_wlo, 3)
                if this and not after:
                    values(0)
                    projection(0)
                    projection(1)
                    projection(2)
                    for q in range(KC):
                        context(q)
                        projection(3 + q)
                    context(3)
                    values(1)
                    for q in range(G):
                        scores(q, (0, 1, 2))
                    values(2)
                    values(3)
                    return
                if this:
                    values(0)
                    values(1)
                    values(2)
                    projection(0)
                if before:
                    context(0)
                if this:
                    values(3)
                for q in range(1, G):
                    if before:
                        context(q)
                    if this:
                        projection(q)
                if this:
                    projection(4)
                    projection(5)
                if first_unit:
                    wlin_transposes(1, x_res)
                if this:
                    scores(0, (0, 1))
                    scores(2, (0, 1))
                if after:
                    transposes(0)
                    transposes(1)
                    transposes(2)
                if this:
                    scores(0, (2,))
                    scores(2, (2,))
                    scores(1, (0, 1, 2))
                if isinstance(pair, int) and k == -1:
                    wlin_transposes(0, c_sb[0])
                if after:
                    adj_transposes()
                if this:
                    scores(3, (0, 1, 2))

            pe.wait_ge(ident_ready, 1)
            for _ in range(8):
                nc.tensor.matmul(ps_u[0][:, 0:P], ident[:, :], ident[:, :], start=True, stop=True)
            run(pe, step)

        @block.scalar
        def _(act):
            def split_hi(piece_out, piece_in):
                nc.scalar.activation(piece_out, piece_in, ACT.Copy).then_inc(act_whi, 1)

            def wlin_hi_parts(l):
                for c in range(KC):
                    act.wait_ge(pe_w, KC * l + c + 1)
                    split_hi(wlin_hi[l][:, c, :], wlin_bank[l][c][:, 0:H])

            def w_hi_parts(l, stage):
                for side in range(2):
                    act.wait_ge(d_w[3 * l + 1 + side], 16)
                    split_hi(w_hi[l][side][:, :, :], stage[side])

            def step(pair, u, this, after, before, before2):
                k = 4 * pair + u
                hb, pb = u % 2, (u + 1) % 2
                first_unit = isinstance(pair, int) and k == 0

                def exponent(p):
                    need(act, dve_us, 2 * (k - 1) + p + 1)
                    nc.scalar.activation(ex[:, p], ex[:, p], ACT.Exp, scale=SCALE).then_inc(act_exp, 1)

                def e_high(p):
                    need(act, pool_e, 2 * (k - 1) + p + 1)
                    need(act, pe_c, 4 * (k - 2) + 2 * p + 2)
                    nc.scalar.activation(e_hi[:, 2 * p:2 * p + 2, :], ex[:, p], ACT.Copy)\
                        .then_inc(act_ehi, 1)

                def v_high(q):
                    n, buf = (k, hb) if this else (k - 1, pb)
                    need(act, dve_vb, 4 * n + q + 1)
                    need(act, pe_c, 4 * (n - 2) + q + 1)
                    nc.scalar.activation(v_hi[buf][:, q, 0:H], vb[:, q % 2, :], ACT.Copy)\
                        .then_inc(act_vhi, 1)

                def c_copy(q):
                    need(act, pe_c, 4 * (k - 1) + q + 1)
                    nc.scalar.activation(c_sb[pb][:, q, :], c_bank(q, this)[:, 0:HV], ACT.Copy)\
                        .then_inc(act_c, 1)

                def n_high(o):
                    ch, side = divmod(o, 2)
                    need(act, pe_n, 6 * k + o + 1)
                    need(act, pe_u, 2 * k)
                    nc.scalar.activation(n_hi[:, ch, :, side, :],
                                         ps_n[o % 2][:, :].rearrange("p (q i) -> p q i", q=G),
                                         ACT.Copy).then_inc(act_nhi, 1)

                def normalize(q):
                    if q == 2:
                        need(act, dve_shift, k)
                    nc.scalar.activation(c_sb[pb][:, q, 0:H], c_sb[pb][:, q, 0:H], ACT.Identity,
                                         bias=shift[:, q:q + 1], scale=gain[:, q:q + 1])\
                        .then_inc(act_norm, 1)

                def h_high(c):
                    need(act, pe_t, 3 * (k + 1) + c + 1)
                    nc.scalar.activation(hT_hi[pb][:, c, :, :],
                                         t_bank[c][:, :].rearrange("p (q i) -> p q i", q=G), ACT.Copy)\
                        .then_inc(act_thi, 1)

                def h_relu(c):
                    if isinstance(pair, int) and k == 1 and c == 0:
                        act.wait_ge(d_small, 16 * 4)
                    need(act, pe_t, 3 * (k + 1) + c + 1)
                    nc.scalar.activation(h_full[:, c, :], t_bank[c][:, :], ACT.Relu,
                                         bias=b0_col[:, c:c + 1], scale=a0_col[:, c:c + 1])\
                        .then_inc(act_h, 1)

                def adj_copy():
                    if u in (0, 3):
                        tp = pair + (u == 3)
                        need(act, pe_at, 2 * tp + pb + 1)
                        need(act, pool_e, 2 * k)
                        nc.scalar.activation(adjT[pb][:, :, :],
                                             ps_t[:, :].rearrange("p (q i) -> p q i", q=G), ACT.Copy)\
                            .then_inc(act_at, 1)

                if first_unit:
                    w_hi_parts(0, [c_sb[1][:, 0:KC, 0:H], y_out[:, 0:KC, :]])
                if not after and u in (3, 0):
                    exponent(0)
                    if this:
                        v_high(0)
                    e_high(0)
                    exponent(1)
                    if this:
                        n_high(0)
                    e_high(1)
                    if this:
                        n_high(1)
                        n_high(2)
                    else:
                        v_high(2)
                        v_high(3)
                    for q in range(G):
                        c_copy(q)
                        if this and q < KC:
                            n_high(3 + q)
                    if this:
                        v_high(1)
                    normalize(2)
                    normalize(3)
                    return
                if before:
                    exponent(0)
                if this:
                    v_high(0)
                if before:
                    e_high(0)
                    exponent(1)
                if this:
                    v_high(1)
                if before:
                    e_high(1)
                if this:
                    v_high(2)
                    n_high(0)
                if before:
                    c_copy(0)
                if this:
                    v_high(3)
                for q in range(1, G):
                    if before:
                        c_copy(q)
                    if this:
                        n_high(q)
                if before:
                    normalize(2)
                if this:
                    n_high(4)
                if before:
                    normalize(3)
                if this:
                    n_high(5)
                if first_unit:
                    wlin_hi_parts(1)
                    w_hi_parts(1, [c_sb[1][:, 0:KC, 0:H], y_out[:, 0:KC, :]])
                if after and u in (0, 3):
                    for c in range(KC):
                        h_high(c)
                    if isinstance(pair, int) and k == -1:
                        wlin_hi_parts(0)
                    adj_copy()
                if after and u in (1, 2):
                    for c in range(KC):
                        h_relu(c)
                    need(act, act_h, 3 * (2 * pair + u))
                    nc.scalar.activation(hT_hi[pb][:, 2, :, :],
                                         h_full[:, 2, :].rearrange("p (q i) -> p q i", q=G), ACT.Copy)\
                        .then_inc(act_thi, 1)

            act.wait_ge(dve_const, 1)
            nc.scalar.activation(warm[:, :], half[:, :], ACT.Exp)
            run(act, step)

        @block.vector
        def _(dve):
            def split_lo(n, piece_out, whole, piece_hi):
                dve.wait_ge(act_whi, n)
                nc.vector.tensor_tensor(piece_out, whole, piece_hi.bitcast(F32), ALU.subtract)\
                    .then_inc(dve_wlo, 1)

            def wlin_lo_parts(l):
                for c in range(KC):
                    split_lo(5 * l + c + 1, wlin_lo[l][:, c, :], wlin_bank[l][c][:, 0:H], wlin_hi[l][:, c, :])

            def w_lo_part(l, side, stage):
                split_lo(5 * l + 4 + side, w_lo[l][side][:, :, :], stage, w_hi[l][side][:, :, :])

            def step(pair, u, this, after, before, before2):
                k = 4 * pair + u
                layer, hb = u // 2, u % 2
                pb = (u + 1) % 2
                first_unit = isinstance(pair, int) and k == 0
                j = 2 * (pair - 1) + u % 2
                i = 2 * pair + (0 if u == 3 else -1)

                def masked(p):
                    need(dve, pe_u, 2 * (k - 1) + p + 1)
                    if p == 0 and u in (1, 2):
                        need(dve, pool_mask, 2 * (2 * pair + u))
                    nc.vector.tensor_tensor(um[:, p].rearrange("p q s i -> p (q s i)"), ps_u[p][:, :],
                                            mask[pb][:, 2 * p:2 * p + 2].rearrange("p q s i -> p (q s i)"),
                                            ALU.mult).then_inc(dve_um, 1)
                    need(dve, dve_um, 2 * (k - 1) + p + 1)
                    need(dve, pool_elo, 2 * (k - 2) + p + 1)
                    nc.vector.tensor_tensor(ex[:, p], um[:, p, :, 0, :], um[:, p, :, 1, :],
                                            ALU.add).then_inc(dve_us, 1)

                def v_bias(q):
                    n = k if this else k - 1
                    need(dve, pe_v, 4 * n + q + 1)
                    need(dve, pool_vlo, 4 * n + q - 1)
                    need(dve, act_vhi, 4 * n + q - 1)
                    nc.vector.tensor_tensor(vb[:, q % 2, :], ps_v[q % 2][:, 0:H],
                                            b_bc[:, layer if this else 1, :], ALU.add).then_inc(dve_vb, 1)

                def n_low(o):
                    ch, side = divmod(o, 2)
                    need(dve, act_nhi, 6 * k + o + 1)
                    nc.vector.tensor_tensor(n_lo[:, ch, :, side, :],
                                            ps_n[o % 2][:, :].rearrange("p (q i) -> p q i", q=G),
                                            n_hi[:, ch, :, side, :].bitcast(F32),
                                            ALU.subtract).then_inc(dve_nlo, 1)

                def stats(q):
                    need(dve, act_c, 4 * (k - 1) + q + 1)
                    nc.vector.bn_stats(bn[:, q, :], c_sb[pb][:, q, 0:H]).then_inc(dve_bn, 1)

                def aggregate():
                    need(dve, dve_bn, 4 * k)
                    need(dve, dve_den2, k - 1)
                    nc.vector.tensor_scalar(den[:, :], c_sb[pb][:, :, H], 1e-10, 1e-3, ALU.add, ALU.mult)\
                        .then_inc(dve_den, 1)
                    for q in range(G):
                        nc.vector.bn_aggr(mv[:, q, :], bn[:, q, :]).then_inc(dve_mv, 1)

                def layernorm_scalars():
                    need(dve, pool_std, k)
                    need(dve, dve_den, k)
                    nc.vector.scalar_tensor_tensor(den2[:, :], std[:, :], BESSEL, den[:, :],
                                                   ALU.mult, ALU.add).then_inc(dve_den2, 1)
                    need(dve, dve_den2, k)
                    need(dve, act_norm, 2 * (k - 1))
                    nc.vector.reciprocal(gain[:, :], den2[:, :]).then_inc(dve_gain, 1)
                    need(dve, dve_gain, k)
                    nc.vector.scalar_tensor_tensor(shift[:, :], mv[:, :, 0], -1.0, gain[:, :],
                                                   ALU.mult, ALU.mult).then_inc(dve_shift, 1)

                def normalize(q):
                    c = c_sb[pb][:, q, 0:H]
                    nc.vector.tensor_scalar(c, c, mv[:, q, 0:1], gain[:, q:q + 1],
                                            ALU.subtract, ALU.mult).then_inc(dve_norm, 1)

                def centre(q):
                    if q == 0:
                        need(dve, dve_mv, 4 * k)
                        if isinstance(pair, int) and k == 3:
                            dve.wait_ge(d_small, 16 * 4)
                    c = c_sb[pb][:, q, 0:H]
                    nc.vector.scalar_tensor_tensor(c, c, mv[:, q, 0:1], a1_bc[:, :],
                                                   ALU.subtract, ALU.mult).then_inc(dve_za, 1)

                def affine(q, group):
                    c = c_sb[group % 2 if isinstance(group, int) else pb][:, q, 0:H]
                    need(dve, dve_za, 2 * group + q + 1)
                    nc.vector.scalar_tensor_tensor(c, c, gain[:, q:q + 1], b1_bc[:, :],
                                                   ALU.mult, ALU.add).then_inc(dve_z, 1)

                def residual(q, j=j, buf=hb):
                    x_of = x_res if this else x_in[buf]
                    if q == 0 and this:
                        need(dve, d_xres, 16 * (j + 1))
                    if q < 2:
                        need(dve, dve_z, 2 * j + q + 1)
                    else:
                        need(dve, pool_z, 2 * j + q - 1)
                    nc.vector.scalar_tensor_tensor(c_sb[buf][:, q, 0:H], c_sb[buf][:, q, 0:H], 0.0,
                                                   x_of[:, q, :], ALU.max, ALU.add).then_inc(dve_y, 1)
                    need(dve, dve_y, 4 * j + q + 1)
                    nc.vector.bn_stats(fbn[:, q, :], c_sb[buf][:, q, 0:H]).then_inc(dve_fbn, 1)

                def final_scalars():
                    for q in range(G):
                        nc.vector.bn_aggr(fmv[:, q, :], fbn[:, q, :]).then_inc(dve_fmv, 1)
                    need(dve, dve_fmv, 4 * (j + 1))
                    nc.vector.tensor_scalar(fvar[:, :], fmv[:, :, 1], 1e-5, None, ALU.add)\
                        .then_inc(dve_fvar, 1)

                def final_apply(q):
                    if q == 0:
                        need(dve, pool_rstd, j + 1)
                        need(dve, d_out, 16 * (j + 1))
                    nc.vector.tensor_scalar(y_out[:, q, :], c_sb[hb][:, q, 0:H], fmv[:, q, 0:1],
                                            rstd[:, q:q + 1], ALU.subtract, ALU.mult)\
                        .then_inc(dve_out, 1)

                high_parts = 8 * pair + (3, 6, 7, 8)[u]

                def h_split(c):
                    src = t_bank[c][:, :] if u in (0, 3) else h_full[:, c, :]
                    src = src.rearrange("p (q i) -> p q i", q=G)
                    hi = hT_hi[pb][:, c, :, :]
                    n = 2 * pair + u - 1
                    if u in (0, 3):
                        need(dve, act_thi, high_parts + c + 1)
                    elif c < 2:
                        need(dve, act_h, 3 * n + c + 1)
                        nc.vector.tensor_copy(hi, src).then_inc(dve_thi, 1)
                        need(dve, dve_thi, 2 * n + c + 1)
                    else:
                        need(dve, act_thi, high_parts + 1)
                    nc.vector.tensor_tensor(hT_lo[pb][:, c, :, :], src, hi.bitcast(F32),
                                            ALU.subtract).then_inc(dve_tlo, 1)

                if first_unit:
                    wlin_lo_parts(0)
                    w_lo_part(0, 0, c_sb[1][:, 0:KC, 0:H])
                    dve.wait_ge(d_bias, 16)
                if not after and u == 1:
                    residual(2)
                    residual(3)
                    dve.wait_ge(dve_fbn, 4 * (j + 1))
                    final_scalars()
                    for q in range(G):
                        final_apply(q)
                    return
                if not after and u in (3, 0):
                    masked(0)
                    if this:
                        v_bias(0)
                    masked(1)
                    if this:
                        for o in range(3):
                            n_low(o)
                        for q in range(KC):
                            stats(q)
                            n_low(3 + q)
                        stats(3)
                        aggregate()
                        v_bias(1)
                        centre(0)
                        centre(1)
                        layernorm_scalars()
                    else:
                        v_bias(2)
                        v_bias(3)
                        affine(0, j)
                        affine(1, j)
                        residual(0)
                        residual(1)
                        for q in range(G):
                            stats(q)
                        aggregate()
                        centre(0)
                        centre(1)
                        layernorm_scalars()
                        affine(0, i)
                        affine(1, i)
                        residual(2)
                        residual(3)
                        dve.wait_ge(dve_fbn, 4 * (j + 1))
                        final_scalars()
                        residual(0, i, pb)
                        residual(1, i, pb)
                        for q in range(G):
                            final_apply(q)
                    return
                if before:
                    masked(0)
                if this:
                    v_bias(0)
                if before:
                    masked(1)
                if this:
                    v_bias(1)
                if first_unit:
                    w_lo_part(0, 1, y_out[:, 0:KC, :])
                if before2:
                    residual(0)
                if this:
                    v_bias(2)
                if before2:
                    residual(1)
                if this:
                    n_low(0)
                if before:
                    stats(0)
                if before2:
                    residual(2)
                if this:
                    v_bias(3)
                if before:
                    stats(1)
                if before2:
                    residual(3)
                    need(dve, dve_fbn, 4 * (j + 1))
                if this:
                    n_low(1)
                if before2:
                    final_scalars()
                if before:
                    stats(2)
                if this:
                    n_low(2)
                if before:
                    stats(3)
                    aggregate()
                if before2:
                    final_apply(0)
                if this:
                    n_low(3)
                if before and u in (0, 3):
                    centre(0)
                    centre(1)
                if before:
                    layernorm_scalars()
                if before and u in (1, 2):
                    normalize(0)
                    normalize(1)
                if before and u in (0, 3):
                    affine(0, i)
                    affine(1, i)
                if before2:
                    final_apply(1)
                if this:
                    n_low(4)
                if before2:
                    final_apply(2)
                if this:
                    n_low(5)
                if before2:
                    final_apply(3)
                if first_unit:
                    wlin_lo_parts(1)
                    w_lo_part(1, 0, c_sb[1][:, 0:KC, 0:H])
                    w_lo_part(1, 1, y_out[:, 0:KC, :])
                if after:
                    for c in range(KC):
                        h_split(c)

            nc.vector.memset(half[:, :], 0.5)
            nc.vector.memset(mhalf[:, :], -0.5)
            for i in range(2):
                nc.vector.memset(v_hi[i][:, :, H:HV].bitcast(F32), 1.0)
                last = nc.vector.memset(v_lo[i][:, :, H:HV].bitcast(F32), 0.0)
            last.then_inc(dve_const, 1)
            run(dve, step)

        @block.gpsimd
        def _(pool):
            def step(pair, u, this, after, before, before2):
                k = 4 * pair + u
                hb, pb = u % 2, (u + 1) % 2
                j = 2 * (pair - 1) + u % 2
                i = 2 * pair + (u - 3) if u == 3 else 2 * pair - 1

                def times_adj(p):
                    need(pool, act_exp, 2 * (k - 1) + p + 1)
                    nc.gpsimd.tensor_tensor(ex[:, p], ex[:, p], adjT[pb][:, 2 * p:2 * p + 2, :], ALU.mult)\
                        .then_inc(pool_e, 1)

                def e_low(p):
                    need(pool, act_ehi, 2 * (k - 1) + p + 1)
                    need(pool, pe_c, 4 * (k - 2) + 2 * p + 2)
                    nc.gpsimd.tensor_tensor(e_lo[:, 2 * p:2 * p + 2, :], ex[:, p],
                                            e_hi[:, 2 * p:2 * p + 2, :].bitcast(F32), ALU.subtract)\
                        .then_inc(pool_elo, 1)

                def v_low(q):
                    n, buf = (k, hb) if this else (k - 1, pb)
                    need(pool, act_vhi, 4 * n + q + 1)
                    nc.gpsimd.tensor_tensor(v_lo[buf][:, q, 0:H], vb[:, q % 2, :],
                                            v_hi[buf][:, q, 0:H].bitcast(F32), ALU.subtract)\
                        .then_inc(pool_vlo, 1)

                def power_rstd():
                    need(pool, dve_fvar, j + 1)
                    nc.gpsimd.tensor_tensor(rstd[:, :], fvar[:, :], mhalf[:, :], ALU.pow)\
                        .then_inc(pool_rstd, 1)

                def power_std():
                    need(pool, dve_mv, 4 * k)
                    nc.gpsimd.tensor_tensor(std[:, :], mv[:, :, 1], half[:, :], ALU.pow)\
                        .then_inc(pool_std, 1)

                def affine(q, group, back):
                    unit = k - 1 - back
                    need(pool, act_norm, 2 * unit + q - 1)
                    z = c_sb[(pb + back) % 2][:, q, 0:H]
                    nc.gpsimd.tensor_tensor(z, z, a1_bc[:, :], ALU.mult).then_inc(pool_za, 1)
                    need(pool, pool_za, 2 * group + q - 1)
                    nc.gpsimd.tensor_tensor(z, z, b1_bc[:, :], ALU.add).then_inc(pool_z, 1)

                if not after and u in (3, 0):
                    times_adj(0)
                    if this:
                        v_low(0)
                    e_low(0)
                    times_adj(1)
                    e_low(1)
                    if not this:
                        v_low(2)
                        v_low(3)
                    if this:
                        power_std()
                        v_low(1)
                    else:
                        affine(2, j, 1)
                        affine(3, j, 1)
                        power_std()
                        affine(2, i, 0)
                        power_rstd()
                        affine(3, i, 0)
                    return
                if before:
                    times_adj(0)
                if this:
                    v_low(0)
                if before:
                    e_low(0)
                    times_adj(1)
                if this:
                    v_low(1)
                if before:
                    e_low(1)
                if this:
                    v_low(2)
                    v_low(3)
                if before2:
                    power_rstd()
                if before:
                    power_std()
                if this and u < 2:
                    need(pool, act_at, 2 * pair + u + 1)
                    need(pool, dve_um, 2 * (k - 1))
                    for side, a in enumerate((adjT[hb], adj_in[hb])):
                        tri = side_of[:, side:side + 1, :].to_broadcast([P, G, P])
                        nc.gpsimd.tensor_tensor(mask[hb][:, :, side, :], a[:, :, :], tri, ALU.mult)\
                            .then_inc(pool_mask, 1)
                if before and u in (0, 3):
                    affine(2, i, 0)
                if before and u in (0, 3):
                    affine(3, i, 0)

            nc.gpsimd.memset(ident[:, :], 0.0).then_inc(pool_fill, 1)
            pool.wait_ge(pool_fill, 1)
            nc.gpsimd.affine_select(out=ident[:, :], in_=ident[:, :], compare_op=ALU.not_equal, fill=1.0,
                                    base=0, pattern=[[-1, P]], channel_multiplier=1).then_inc(ident_ready, 1)
            nc.gpsimd.memset(side_of[:, :, :], 1.0).then_inc(pool_fill, 1)
            pool.wait_ge(pool_fill, 2)
            nc.gpsimd.affine_select(out=side_of[:, 0, :], in_=side_of[:, 0, :], pattern=[[-1, P]],
                                    compare_op=ALU.is_ge, fill=0.0, base=0, channel_multiplier=1)\
                .then_inc(tri_ready, 1)
            nc.gpsimd.affine_select(out=side_of[:, 1, :], in_=side_of[:, 1, :], pattern=[[1, P]],
                                    compare_op=ALU.is_gt, fill=0.0, base=0, channel_multiplier=-1)\
                .then_inc(tri_ready, 1)
            pool.wait_ge(tri_ready, 2)
            pool.wait_ge(dve_const, 1)
            pool.wait_ge(d_small, 16 * 4)
            run(pool, step)


_INS = ["x", "adj", "L0_gnn_W_left", "L0_gnn_W_right", "L0_gnn_W_lin", "L0_gnn_b_lin", "L0_gnn_ln_a",
        "L0_gnn_ln_b"]


def kernel(**inputs):
    import numpy as _np
    import concourse.bacc as _bacc
    from concourse import mybir as _mybir
    from concourse.bass_utils import run_bass_kernel_spmd as _run

    nc = _bacc.Bacc("TRN2", target_bir_lowering=False, num_devices=1)
    arrays, args = {}, []
    for name in _INS:
        a = _np.ascontiguousarray(inputs[name])
        arrays[f"in_{name}_dram"] = a
        args.append(nc.dram_tensor(f"in_{name}_dram", a.shape, _mybir.dt.from_np(a.dtype),
                                   kind="ExternalInput").ap())
    out_shape = tuple(inputs["x"].shape)
    args.append(nc.dram_tensor("out_0_dram", out_shape, _mybir.dt.float32, kind="ExternalOutput").ap())
    gnn_resnorm_kernel(nc, *args)
    r = _run(nc, [arrays], core_ids=[0])
    return r.results[0]["out_0_dram"]
```
